# Optimizing a Trainium2 kernel written in Bass

```python
import numpy as np
import jax
import jax.numpy as jnp

def _softmax(x, axis=-1):
    return jax.nn.softmax(x, axis=axis)

def _gelu(x):
    return jax.nn.gelu(x, approximate=True)

def _silu(x):
    return jax.nn.silu(x)

def _sigmoid(x):
    return jax.nn.sigmoid(x)

def _layernorm(x, axis=-1, eps=1e-05):
    m = jnp.mean(x, axis=axis, keepdims=True)
    v = jnp.var(x, axis=axis, keepdims=True)
    return (x - m) / jnp.sqrt(v + eps)

def _scatter_add(tgt, idx, src, axis=0):
    return tgt.at[idx].add(src)

def _segment_sum(src, seg, n):
    return jax.ops.segment_sum(src, seg, n)
kernel_name = 'mk_adaln_d1_jaxref_r4_58890e'

def setup_inputs(seed: int=0):
    np.random.seed(seed)
    _w = jnp.asarray

    def _L0_attn_setup():
        import jax, jax.numpy as jnp
        import numpy as np
        B, T, EMB, HEADS = (4, 512, 256, 16)
        CHUNK = EMB // HEADS
        key = jax.random.key(seed)
        kx, kq, kk, kv, ku = jax.random.split(key, 5)
        s = CHUNK ** (-0.5)
        return {'x': jax.random.normal(kx, (B, T, EMB), jnp.float32), 'Wq': jax.random.normal(kq, (CHUNK, CHUNK), jnp.float32) * s, 'Wk': jax.random.normal(kk, (CHUNK, CHUNK), jnp.float32) * s, 'Wv': jax.random.normal(kv, (CHUNK, CHUNK), jnp.float32) * s, 'Wu': jax.random.normal(ku, (EMB, EMB), jnp.float32) * EMB ** (-0.5), 'bu': jnp.zeros((EMB,), jnp.float32)}
    _L0_attn_in = _L0_attn_setup()

    def _L0_ffn_setup():
        import jax, jax.numpy as jnp
        import numpy as np
        E = 16
        K = 4
        NG = 4
        TG = 2
        SCALE = 2.5
        NORM_TOPK = True
        H = 256
        I = 128
        SH_I = I * 2
        B, S = (2, 512)
        key = jax.random.key(seed)
        ks = jax.random.split(key, 9)

        def w(k, shape, fan_in):
            return jax.random.normal(k, shape, jnp.float32) * (1.0 / np.sqrt(fan_in))
        return {'hidden_states': jax.random.normal(ks[0], (B, S, H), jnp.float32), 'gate_w': w(ks[1], (E, H), H), 'gate_bias': jnp.zeros((E,), jnp.float32), 'Wg': w(ks[2], (E, I, H), H), 'Wu': w(ks[3], (E, I, H), H), 'Wd': w(ks[4], (E, H, I), I), 'Ws_g': w(ks[5], (SH_I, H), H), 'Ws_u': w(ks[6], (SH_I, H), H), 'Ws_d': w(ks[7], (H, SH_I), SH_I)}
    _L0_ffn_in = _L0_ffn_setup()
    _L0_c = _w((lambda *s: np.random.randn(*s).astype(np.float32) * 0.05)(1, 256))
    _L0_wmod = _w((lambda *s: np.random.randn(*s).astype(np.float32) * 0.05)(256, 6 * 256) * 256 ** (-0.5))
    _d = {'L0_attn_x': _L0_attn_in['x'], 'L0_attn_Wq': _L0_attn_in['Wq'], 'L0_attn_Wk': _L0_attn_in['Wk'], 'L0_attn_Wv': _L0_attn_in['Wv'], 'L0_attn_Wu': _L0_attn_in['Wu'], 'L0_attn_bu': _L0_attn_in['bu'], 'L0_ffn_gate_w': _L0_ffn_in['gate_w'], 'L0_ffn_gate_bias': _L0_ffn_in['gate_bias'], 'L0_ffn_Wg': _L0_ffn_in['Wg'], 'L0_ffn_Wu': _L0_ffn_in['Wu'], 'L0_ffn_Wd': _L0_ffn_in['Wd'], 'L0_ffn_Ws_g': _L0_ffn_in['Ws_g'], 'L0_ffn_Ws_u': _L0_ffn_in['Ws_u'], 'L0_ffn_Ws_d': _L0_ffn_in['Ws_d'], 'L0_c': _L0_c, 'L0_wmod': _L0_wmod}
    _x0 = _d['L0_attn_x']
    _d['L0_attn_x'] = jax.random.normal(jax.random.fold_in(jax.random.key(seed), 1), (1, 4096, 256), dtype=_x0.dtype)
    del _x0
    return _d

def reference(L0_attn_x, L0_attn_Wq, L0_attn_Wk, L0_attn_Wv, L0_attn_Wu, L0_attn_bu, L0_ffn_gate_w, L0_ffn_gate_bias, L0_ffn_Wg, L0_ffn_Wu, L0_ffn_Wd, L0_ffn_Ws_g, L0_ffn_Ws_u, L0_ffn_Ws_d, L0_c, L0_wmod):

    def _L0_attn_ref(x, Wq, Wk, Wv, Wu, bu):
        import jax, jax.numpy as jnp
        import numpy as np
        B, T, EMB, HEADS = (4, 512, 256, 16)
        CHUNK = EMB // HEADS
        b, t, d = x.shape
        h = HEADS
        c = d // h
        xh = x.reshape(b, t, h, c)
        scale = d ** (-0.25)
        q = jnp.einsum('bthc,oc->btho', xh, Wq) * scale
        k = jnp.einsum('bthc,oc->btho', xh, Wk) * scale
        v = jnp.einsum('bthc,oc->btho', xh, Wv)
        scores = jnp.einsum('bihc,bjhc->bhij', q, k)
        i = jnp.arange(t)[:, None]
        j = jnp.arange(t)[None, :]
        scores = jnp.where(j > i, -jnp.inf, scores)
        attn = jax.nn.softmax(scores, axis=-1)
        y = jnp.einsum('bhij,bjhc->bihc', attn, v).reshape(b, t, d)
        return y @ Wu.T + bu

    def _L0_ffn_ref(hidden_states, gate_w, gate_bias, Wg, Wu, Wd, Ws_g, Ws_u, Ws_d):
        import jax, jax.numpy as jnp
        import numpy as np
        E = 16
        K = 4
        NG = 4
        TG = 2
        SCALE = 2.5
        NORM_TOPK = True
        H = 256
        I = 128
        SH_I = I * 2
        B, S = (2, 512)
        x = hidden_states
        b, s, h = x.shape
        n = b * s
        xf = x.reshape(n, h)
        logits = xf @ gate_w.T
        scores = jax.nn.sigmoid(logits)
        sfc = scores + gate_bias
        epg = E // NG
        grp = sfc.reshape(n, NG, epg)
        g_scores = jax.lax.top_k(grp, 2)[0].sum(-1)
        _, gidx = jax.lax.top_k(g_scores, TG)
        gmask = jax.nn.one_hot(gidx, NG, dtype=sfc.dtype).sum(1)
        emask = jnp.repeat(gmask, epg, axis=1)
        masked = jnp.where(emask > 0, sfc, -jnp.inf)
        _, topk_idx = jax.lax.top_k(masked, K)
        topk_w = jnp.take_along_axis(scores, topk_idx, axis=1)
        if K > 1 and NORM_TOPK:
            topk_w = topk_w / (topk_w.sum(-1, keepdims=True) + 1e-20)
        topk_w = topk_w * SCALE
        cw = (jax.nn.one_hot(topk_idx, E, dtype=topk_w.dtype) * topk_w[..., None]).sum(1)
        hg = jnp.einsum('nh,eih->nei', xf, Wg)
        hu = jnp.einsum('nh,eih->nei', xf, Wu)
        act = jax.nn.silu(hg) * hu
        y = jnp.einsum('nei,ne,ehi->nh', act, cw, Wd)
        shared = jax.nn.silu(xf @ Ws_g.T) * (xf @ Ws_u.T) @ Ws_d.T
        y = y + shared
        return (x + y.reshape(b, s, h)).astype(hidden_states.dtype)
    x = L0_attn_x
    mod = (_silu(L0_c) @ L0_wmod).reshape(L0_c.shape[0], 6, 1, -1)
    sa, ca, ga, sb, cb, gb = (mod[:, 0], mod[:, 1], mod[:, 2], mod[:, 3], mod[:, 4], mod[:, 5])
    ga = (2 * (ga >= 0) - 1) * jnp.maximum(jnp.abs(ga), 0.25)
    gb = (2 * (gb >= 0) - 1) * jnp.maximum(jnp.abs(gb), 0.25)
    h = _layernorm(x, axis=-1) * (1 + ca) + sa
    x = x + ga * _L0_attn_ref(h, L0_attn_Wq, L0_attn_Wk, L0_attn_Wv, L0_attn_Wu, L0_attn_bu)
    h = _layernorm(x, axis=-1) * (1 + cb) + sb
    x = x + gb * _L0_ffn_ref(h, L0_ffn_gate_w, L0_ffn_gate_bias, L0_ffn_Wg, L0_ffn_Wu, L0_ffn_Wd, L0_ffn_Ws_g, L0_ffn_Ws_u, L0_ffn_Ws_d)
    return x

_drawn_inputs = setup_inputs


def setup_inputs(seed=0):
    import zlib

    import numpy as np

    out = dict(_drawn_inputs(seed))
    spreads = {'L0_attn_bu': (0.0, 0.1), 'L0_ffn_gate_bias': (0.0, 0.1)}
    factors = {}
    for name, (base, spread) in spreads.items():
        noise = np.random.default_rng([zlib.crc32(name.encode()), seed]).standard_normal(out[name].shape)
        drawn = base * np.exp(spread * noise) if base else spread * noise
        out[name] = jnp.asarray(drawn.astype(out[name].dtype))
    for name, factor in factors.items():
        out[name] = (out[name] * factor).astype(out[name].dtype)
    return out
```

```python
from contextlib import ExitStack

import concourse.bass as bass
from concourse import mybir

F32 = mybir.dt.float32
F32R = mybir.dt.float32r
BF16 = mybir.dt.bfloat16
ALU = mybir.AluOpType
ACT = mybir.ActivationFunctionType
AX_X = mybir.AxisListType.X

P = 128
T = 4096
D = 256
H = 16
C = D // H
NS = D // P
NT = T // P
BW = 512
NB = T // BW
TPB = BW // P
EPS = 1e-5
MASKED = -1e30
FLOOR = 0.25
HPAD = H + 1

QPARTS = (0, 0, 0, 1, 1, 2)
KPARTS = (0, 1, 2, 0, 1, 0)
ROWS = C * len(QPARTS)
SROWS = ROWS + 2

E = 16
TOPK = 4
NG = 4
TG = 2
RSCALE = 2.5
I = 128
U = E + 2
WU = 2 * NS * I + D

LEAD = 5
SW = 1
S_SLOTS = 3
ST_SLOTS = 3
M_SLOTS = 4


def prepare(nc, t, d):
    with ExitStack() as ctx:
        def sb(name, shape, dt):
            return ctx.enter_context(nc.sbuf_tensor(name, shape, dt))

        def sem(name):
            return ctx.enter_context(nc.semaphore(name))

        QKR = 4
        wmod = sb("wmod", [P, NS, 6 * D], F32)
        ccol = sb("ccol", [P, NS], F32)
        scol = sb("scol", [P, NS], F32)
        wrep = sb("wrep", [P, 3, C], F32)
        onb = sb("onb", [P, P // C, C], F32)
        wbd = sb("wbd", [P, 3, P], F32)
        hT = t["h2"]
        xn = sb("xn", [P, 2, TPB, D], F32)
        stats = sb("stats", [P, NT, 6], F32)
        mv = sb("mv", [P, NT, 2], F32)
        ve = sb("ve", [P, NT], F32)
        rstd = sb("rstd", [P, NT], F32)
        half = sb("half", [P, NT], F32)
        grow = sb("grow", [1, 2 * D], F32)
        gtmp = sb("gtmp", [1, 3, D], F32)
        burow = sb("burow", [1, D], F32)
        gbt = sb("gbt", [P, 3, NS], F32)
        ones1 = sb("ones1", [1, P], F32)
        parts = sb("parts", [P, QKR, 3, BW], BF16)
        rest = sb("rest", [P, QKR, BW], F32)
        tp = [ctx.enter_context(nc.psum_tensor(f"tp{i}", [P, BW], F32)) for i in range(2)]
        qk = [ctx.enter_context(nc.psum_tensor(f"qk{i}", [P, BW], F32)) for i in range(QKR)]
        vp = [ctx.enter_context(nc.psum_tensor(f"vp{i}", [P, BW], F32)) for i in range(2)]

        s_c, s_wm, s_wr, s_bu = sem("c_in"), sem("wmod_in"), sem("wrep_in"), sem("bu_in")
        s_x = [sem(f"x_in{g}") for g in range(4)]
        s_store = [sem(f"parts_out{i}") for i in range(QKR)]
        s_zero = sem("zero_rows_out")
        s_pool, s_const, s_dve = sem("pool_chain"), sem("constants"), sem("dve_chain")
        s_silu, s_modp, s_mod = sem("silu_c"), sem("mod_psum"), sem("mod_ready")
        s_grow, s_bc, s_ve, s_rstd, s_xn = sem("ga_row"), sem("ga_bcast"), sem("ve"), sem("rstd"), sem("xn")
        s_tp, s_hT, s_wbd = sem("transposed"), sem("hT_ready"), sem("wbd_ready")
        s_qk, s_p1, s_r, s_p2, s_p3 = sem("qk_psum"), sem("part1"), sem("rest"), sem("part2"), sem("part3")
        s_v, s_vc = sem("v_psum"), sem("v_copied")
        GT = NT // 4
        chunks = [(b, s, w) for b in range(NB) for s in range(NS) for w in range(2)]
        modp = vp[0]

        with nc.Block() as block:
            @block.sync
            def _(sp):
                xv = d["x"].rearrange("a (n p) c -> p (a n) c", p=P)
                sp.dma_start(ccol[:, :], d["c"].rearrange("a (s p) -> p (a s)", p=P),
                             allow_slow_non_contiguous=True).then_inc(s_c, 16)
                sp.dma_start(wmod[:, :, :], d["wmod"].rearrange("(s p) n -> p s n", p=P)).then_inc(s_wm, 16)
                for g in range(4):
                    sp.dma_start(t["x"][:, g * GT:(g + 1) * GT, :], xv[:, g * GT:(g + 1) * GT, :]).then_inc(s_x[g], 16)
                sp.wait_ge(s_const, 1)
                for which in ("qs", "ks"):
                    for k in range(3):
                        sp.dma_start(d[which][k, D:HPAD * C, :], t["qst"][0][0:C, :]).then_inc(s_zero, 16)
                for c, (b, s, w) in enumerate(chunks):
                    sp.wait_ge(s_p3, c + 1)
                    dst = d["ks" if w else "qs"][:, s * P:(s + 1) * P, b * BW:(b + 1) * BW]
                    sp.dma_start(dst.rearrange("k p n -> p k n"), parts[:, c % QKR, :, :]).then_inc(s_store[c % QKR], 16)
                for i in range(QKR):
                    sp.wait_ge(s_store[i], 16 * len(chunks) // QKR)
                sp.wait_ge(s_zero, 96)

            @block.gpsimd
            def _(pool):
                n = [0]

                def link(ins):
                    n[0] += 1
                    ins.then_inc(s_pool, 1)
                    pool.wait_ge(s_pool, n[0])

                link(pool.memset(t["qst"][0][0:C, :], 0.0))
                pool.memset(half[:, :], -0.5).then_inc(s_const, 1)
                link(pool.memset(t["identf"][:, :], 0.0))
                link(pool.affine_select(out=t["identf"][:, :], in_=t["identf"][:, :], compare_op=ALU.not_equal,
                                        fill=1.0, base=0, pattern=[[-1, P]], channel_multiplier=1))
                link(pool.memset(onb[:, :, :], 1.0))
                link(pool.affine_select(out=onb[:, :, :], in_=onb[:, :, :], compare_op=ALU.is_ge, fill=0.0,
                                        base=0, pattern=[[-C, P // C], [0, C]], channel_multiplier=1))
                link(pool.affine_select(out=onb[:, :, :], in_=onb[:, :, :], compare_op=ALU.is_ge, fill=0.0,
                                        base=C - 1, pattern=[[C, P // C], [0, C]], channel_multiplier=-1))
                link(pool.memset(ones1[:, :], 1.0))
                link(pool.memset(t["maskq"][:, :], 0.0))
                link(pool.affine_select(out=t["maskq"][:, :], in_=t["maskq"][:, :], compare_op=ALU.is_ge,
                                        fill=MASKED, base=0, pattern=[[-1, P]], channel_multiplier=1))
                link(pool.memset(t["maskk"][:, :], 0.0))
                link(pool.affine_select(out=t["maskk"][:, :], in_=t["maskk"][:, :], compare_op=ALU.is_ge,
                                        fill=MASKED, base=0, pattern=[[1, P]], channel_multiplier=-1))
                link(pool.memset(t["v"][:, :, D:HPAD * C], 0.0))
                for i in range(2):
                    link(pool.memset(t["vpad"][i][:, :, C:32], 0.0))
                    link(pool.memset(t["vpad"][i][:, :, C:C + 1], 1.0))
                    link(pool.memset(t["kst"][i][ROWS:P, :], 1.0))
                    link(pool.memset(t["qst"][i][ROWS:P, :], 0.0))
                pool.memset(half[:, :], -0.5).then_inc(s_const, 1)
                pool.wait_ge(s_const, 2)
                for g in range(4):
                    pool.wait_ge(s_ve, g + 1)
                    c0, c1 = g * GT, (g + 1) * GT
                    pool.tensor_tensor(rstd[:, c0:c1], ve[:, c0:c1], half[:, c0:c1], ALU.pow).then_inc(s_rstd, 1)
                for c in range(len(chunks)):
                    pool.wait_ge(s_p2, c + 1)
                    i = c % QKR
                    pool.tensor_tensor(parts[:, i, 2, :], rest[:, i, :], parts[:, i, 1, :],
                                       ALU.subtract).then_inc(s_p3, 1)

            @block.vector
            def _(dve):
                n = [0]

                def link(ins):
                    n[0] += 1
                    ins.then_inc(s_dve, 1)
                    dve.wait_ge(s_dve, n[0])

                dve.wait_ge(s_const, 2)
                link(dve.tensor_copy(t["identb"][:, :], t["identf"][:, :]))
                link(dve.tensor_tensor(t["sel"][:, :], t["identf"][:, 0:32], t["identf"][:, 32:64], ALU.add))
                link(dve.tensor_tensor(t["sel"][:, :], t["sel"][:, :], t["identf"][:, 64:96], ALU.add))
                link(dve.tensor_tensor(t["sel"][:, :], t["sel"][:, :], t["identf"][:, 96:128], ALU.add))
                dve.wait_ge(s_wr, 16 * 3 * P // C)
                scale = float(D) ** -0.25
                for w in range(3):
                    ins = dve.scalar_tensor_tensor(
                        out=wbd[:, w, :].rearrange("p (h o) -> p h o", o=C), in0=onb[:, :, :],
                        scalar=scale if w < 2 else 1.0, in1=wrep[:, w, :].unsqueeze(1).broadcast_to([P, P // C, C]),
                        op0=ALU.mult, op1=ALU.mult)
                ins.then_inc(s_wbd, 1)

                def modulation():
                    dve.wait_ge(s_modp, 1)
                    link(dve.tensor_copy(t["mod"][:, :], modp[:, 0:12]))
                    for j in (1, 4):
                        link(dve.tensor_scalar(t["mod"][:, 2 * j:2 * j + 2], t["mod"][:, 2 * j:2 * j + 2],
                                               1.0, None, ALU.add))
                    floor_gate(t["mod"][:, 10:12], gbt)
                    link(dve.tensor_copy(t["gb"][:, :], gbt[:, 0, :]))
                    link(dve.tensor_copy(gtmp[:, 0, :], modp[0:1, 16:16 + D]))
                    floor_gate(gtmp[:, 0, :], gtmp)
                    link(dve.tensor_copy(grow[:, 0:D], gtmp[:, 0, :]))
                    dve.wait_ge(s_bu, 16)
                    dve.tensor_tensor(grow[:, D:2 * D], gtmp[:, 0, :], burow[:, :], ALU.mult).then_inc(s_mod, 1)

                def floor_gate(src, b):
                    link(dve.tensor_scalar(b[:, 1, :], src, -1.0, None, ALU.mult))
                    link(dve.tensor_tensor(b[:, 1, :], b[:, 1, :], src, ALU.max))
                    link(dve.tensor_scalar(b[:, 2, :], src, 0.0, 2.0, ALU.is_ge, ALU.mult))
                    link(dve.tensor_scalar(b[:, 2, :], b[:, 2, :], -1.0, None, ALU.add))
                    link(dve.tensor_scalar(b[:, 1, :], b[:, 1, :], FLOOR, None, ALU.max))
                    link(dve.tensor_tensor(b[:, 0, :], b[:, 1, :], b[:, 2, :], ALU.mult))

                for g in range(4):
                    dve.wait_ge(s_x[g], 16)
                    ts = range(g * GT, (g + 1) * GT)
                    for i in ts:
                        ins = dve.bn_stats(stats[:, i, :], t["x"][:, i, :])
                    link(ins)
                    for i in ts:
                        ins = dve.bn_aggr(mv[:, i, :], stats[:, i, :])
                    link(ins)
                    dve.tensor_scalar(ve[:, ts[0]:ts[-1] + 1], mv[:, ts[0]:ts[-1] + 1, 1], EPS, None,
                                      ALU.add).then_inc(s_ve, 1)
                    if g == 0:
                        modulation()
                    dve.wait_ge(s_rstd, g + 1)
                    for i in ts:
                        if i % TPB == 0 and i >= 2 * TPB:
                            dve.wait_ge(s_tp, NS * (i // TPB - 1))
                        dve.tensor_scalar(xn[:, i // TPB % 2, i % TPB, :], t["x"][:, i, :], mv[:, i, 0:1], rstd[:, i:i + 1],
                                          ALU.subtract, ALU.mult).then_inc(s_xn, 1)
                dve.wait_ge(s_bc, 1)
                link(dve.tensor_copy(t["gab"][:, :], modp[:, 0:BW]))
                for i in range(NT):
                    ins = dve.tensor_tensor(t["x"][:, i, :], t["x"][:, i, :], t["gab"][:, D:2 * D], ALU.add)
                ins.then_inc(s_mod, 1)
                for c in range(len(chunks)):
                    i = c % QKR
                    dve.wait_ge(s_p1, c + 1)
                    if c >= QKR:
                        dve.wait_ge(s_p3, c - QKR + 1)
                    dve.tensor_tensor(rest[:, i, :], qk[i][:, :], parts[:, i, 0, :], ALU.subtract).then_inc(s_r, 1)

            @block.scalar
            def _(act):
                for w, name in enumerate(("WqT", "WkT", "WvT")):
                    for h in range(P // C):
                        act.dma_start(wrep[h * C:(h + 1) * C, w, :], d[name]).then_inc(s_wr, 16)
                act.dma_start(burow[:, :], d["bu"].rearrange("(a n) -> a n", a=1)).then_inc(s_bu, 16)
                act.wait_ge(s_c, 16)
                act.activation(scol[:, :], ccol[:, :], ACT.Silu).then_inc(s_silu, 1)
                act.wait_ge(s_mod, 1)
                for c in range(2 * NB):
                    b, s = divmod(c, NS)
                    act.wait_ge(s_tp, c + 1)
                    act.activation(hT[:, b, s, :], tp[c % 2][:, :], ACT.Identity,
                                   scale=t["mod"][:, 2 + s:3 + s], bias=t["mod"][:, s:s + 1]).then_inc(s_hT, 1)

                def part2(c):
                    i = c % QKR
                    act.wait_ge(s_r, c + 1)
                    act.activation(parts[:, i, 1, :], rest[:, i, :], ACT.Copy).then_inc(s_p2, 1)

                for c in range(len(chunks)):
                    i = c % QKR
                    act.wait_ge(s_qk, c + 1)
                    if c >= QKR:
                        act.wait_ge(s_store[i], 16 * (c // QKR))
                    act.activation(parts[:, i, 0, :], qk[i][:, :], ACT.Copy).then_inc(s_p1, 1)
                    if c >= 1:
                        part2(c - 1)
                part2(len(chunks) - 1)
                for c in range(NT // 2):
                    act.wait_ge(s_v, c + 1)
                    act.activation(t["v"][:, 2 * c:2 * c + 2, 0:D],
                                   vp[c % 2][:, :].rearrange("p (a n) -> p a n", a=2), ACT.Copy).then_inc(s_vc, 1)

            @block.tensor
            def _(pe):
                pe.wait_ge(s_silu, 1)
                pe.wait_ge(s_wm, 16)
                for j in range(12):
                    for s in range(NS):
                        pe.matmul(modp[:, j:j + 1], wmod[:, s, j * P:(j + 1) * P], scol[:, s:s + 1],
                                  start=(s == 0), stop=(s == NS - 1))
                for s in range(NS):
                    ins = pe.matmul(modp[0:1, 16:16 + D], scol[:, s:s + 1], wmod[:, s, 2 * D:3 * D],
                                    start=(s == 0), stop=(s == NS - 1))
                ins.then_inc(s_modp, 1)
                pe.wait_ge(s_const, 2)
                for c in range(2 * NB):
                    b, s = divmod(c, NS)
                    pe.wait_ge(s_xn, TPB * (b + 1))
                    if c >= 2:
                        pe.wait_ge(s_hT, c - 1)
                    for i in range(TPB):
                        ins = pe.transpose(tp[c % 2][:, i * P:(i + 1) * P],
                                           xn[:, b % 2, i, s * P:(s + 1) * P], t["identf"][:, :])
                    ins.then_inc(s_tp, 1)
                pe.wait_ge(s_mod, 1)
                pe.matmul(modp[:, :], ones1[:, :], grow[:, :], start=True, stop=True).then_inc(s_bc, 1)
                pe.wait_ge(s_wbd, 1)
                for c, (b, s, w) in enumerate(chunks):
                    if c % 4 == 0:
                        pe.wait_ge(s_hT, 2 * b + 2)
                    if c >= QKR:
                        pe.wait_ge(s_r, c - QKR + 1)
                    pe.matmul(qk[c % QKR][:, :], wbd[:, w, :], hT[:, b, s, :],
                              start=True, stop=True).then_inc(s_qk, 1)
                pe.wait_ge(s_mod, 2)
                for c in range(NT // 2):
                    if c >= 2:
                        pe.wait_ge(s_vc, c - 1)
                    for i in range(2):
                        for s in range(NS):
                            n = 2 * c + i
                            ins = pe.matmul(vp[c % 2][:, i * D + s * P:i * D + (s + 1) * P],
                                            hT[:, n // TPB, s, n % TPB * P:(n % TPB + 1) * P], wbd[:, 2, :], start=True, stop=True)
                    ins.then_inc(s_v, 1)


PV_LAG, YO_LAG, MT_LAG = 6, 5, 9


def tile_jobs(slot, j):
    jobs = []
    for r in range(TPB):
        keys = (TPB * j + r + 1) * P
        for c in range(-(-keys // (SW * BW))):
            jobs.append((slot, j, r, c, c * SW * BW, min(keys, (c + 1) * SW * BW)))
    return jobs


def schedule(heads, blocks):
    units = [(slot, j, k) for slot in heads for j in range(NB) for k in range(TPB * (j + 1))]
    jobs = [(x, q == len(js) - 1) for slot, j in blocks for js in [tile_jobs(slot, j)] for q, x in enumerate(js)]
    work = [(x[5] - x[4]) + 200 for x, _ in jobs]
    events, later, done, sent = [], [], 0, 0
    n_steps = len(units) + PV_LAG + YO_LAG
    total = max(1, len(units))
    for s in range(n_steps if units else 1):
        events += [e for at, e in later if at == s]
        later = [(at, e) for at, e in later if at != s]
        if s < len(units):
            slot, j, k = units[s]
            early = [e for _, e in later if k == 0 and e == ("MT", (slot, j))]
            events += early
            later = [(at, e) for at, e in later if e not in early]
            events.append(("ST", (s, slot, j, k)))
            if k == TPB * (j + 1) - 1 and j == NB - 1:
                later.append((s + 3, ("FREE", slot)))
            if k == 3 and j == 3:
                later.append((s + 1, ("V", 1 - slot)))
        g = s - PV_LAG
        if g >= 0 and g % 4 == 0 and g < len(units):
            slot, j, k = units[g]
            events.append(("PV", (g // 4, slot, j, k // TPB)))
            if k // TPB == j:
                later += [(s + 1, ("OD", (slot, j))), (s + YO_LAG, ("YO", (slot, j)))]
        while sent < len(jobs) and (not units or done <= sum(work) * (s + 1) / total):
            x, last = jobs[sent]
            if last:
                due = [e for _, e in later if e[0] == "MT"][:-(M_SLOTS - 2)]
                events += due
                later = [(at, e) for at, e in later if e not in due]
            events.append(("S", (sent, x, last)))
            done += work[sent]
            sent += 1
            if last:
                later.append((s + MT_LAG, ("MT", (x[0], x[1]))))
    events += [e for _, e in sorted(later, key=lambda z: z[0])]
    assert sent == len(jobs)
    return events


class Section:

    def __init__(self):
        self.n = {}

    def add(self, name, by=1):
        self.n[name] = self.n.get(name, 0) + by
        return self.n[name]

    def get(self, name):
        return self.n.get(name, 0)


def attend(nc, t, d):
    with ExitStack() as ctx:
        def sb(name, shape, dt):
            return ctx.enter_context(nc.sbuf_tensor(name, shape, dt))

        NP = 8
        prob = sb("prob", [P, NP, BW], F32)
        mx = sb("mx", [P, M_SLOTS, TPB, NB // SW], F32)
        mq = sb("mq", [P, M_SLOTS, TPB], F32)
        nm = sb("nm", [P, M_SLOTS, TPB], F32)
        mt = sb("mt", [P, M_SLOTS, TPB, 2], BF16)
        od = sb("od", [P, 2, BW], F32)
        rl = sb("rl", [P, 2, TPB], F32)
        tok = sb("tok", [1, 2], F32)
        S = [ctx.enter_context(nc.psum_tensor(f"S{i}", [P, SW * BW], F32)) for i in range(S_SLOTS)]
        ST = [ctx.enter_context(nc.psum_tensor(f"ST{i}", [P, BW], F32)) for i in range(ST_SLOTS)]
        O = ctx.enter_context(nc.psum_tensor("O", [P, BW], F32))
        M = ctx.enter_context(nc.psum_tensor("M", [P, BW], F32))
        names = ("s_full", "s_read", "s_last_read", "st_full", "exp_done", "pv_done", "od_done", "m_full",
                 "m_split", "mt_full", "m_copied", "y_full", "y_done", "v_full", "dve_chain", "pool_chain",
                 "heads_free", "stack0", "stack1", "y_chain")
        q = {n: ctx.enter_context(nc.semaphore("at_" + n)) for n in names}
        qst, kst, vpad = t["qst"], t["kst"], t["vpad"]

        first = [(0, j) for j in range(LEAD)]
        body = [(0, j) for j in range(LEAD, NB)] + [(1, j) for j in range(NB)] + first
        sections = {"first": schedule([], first), "body": schedule([0, 1], body)}

        def settle(eng, sec, mine):
            for n in mine:
                if sec.get(n):
                    eng.wait_ge(q[n], sec.get(n))
            eng.drain()
            for n in mine:
                if sec.get(n):
                    eng.nop().then_inc(q[n], -sec.get(n))

        LOADED = 16 * (len(QPARTS) + len(KPARTS))

        def load(sp, slot, head):
            row = head * C
            for name, st, parts in (("qs", qst[slot], QPARTS), ("ks", kst[slot], KPARTS)):
                for i, k in enumerate(parts):
                    sp.dma_start(st[i * C:(i + 1) * C, :], d[name][k, bass.ds(row, C), :]
                                 ).then_inc(q[f"stack{slot}"], 16)

        with nc.Block() as block:
            @block.sync
            def _(sp):
                load(sp, 0, 0)
                sp.sem_inc(q["heads_free"], 1)
                with sp.Fori(0, H // 2) as pair:
                    h = pair * 2
                    for n, slot in enumerate((1, 0)):
                        sp.wait_ge(q["heads_free"], n + 1)
                        load(sp, slot, h + 1 + n)
                    sp.drain()
                    sp.nop().then_inc(q["heads_free"], -2)

            @block.tensor
            def _(pe):
                def section(name):
                    sec = Section()
                    pending = []
                    groups = outs = 0
                    mrow = {}
                    if name == "first":
                        sec.add("stack0", LOADED)
                        pe.wait_ge(q["stack0"], LOADED)
                        sec.add("v_full")
                    for kind, e in sections[name]:
                        if kind == "S":
                            n, (slot, j, r, c, k0, k1), last = e
                            if name == "body" and j == 0 and r == 0:
                                sec.add(f"stack{slot}", LOADED)
                                pe.wait_ge(q[f"stack{slot}"], LOADED)
                            if n >= S_SLOTS:
                                pe.wait_ge(q[pending[-S_SLOTS][0]], pending[-S_SLOTS][1])
                            src = "s_last_read" if last else "s_read"
                            pending.append((src, sec.add(src)))
                            qc = (TPB * j + r) * P
                            for a in range(k0, k1, BW):
                                b = min(a + BW, k1)
                                diag = b == qc + P
                                ins = pe.matmul(S[n % S_SLOTS][:, a - k0:b - k0], qst[slot][0:ROWS, qc:qc + P],
                                                kst[slot][0:ROWS, a:b], start=True, stop=not diag)
                                if diag:
                                    ins = pe.matmul(S[n % S_SLOTS][:, b - P - k0:b - k0], t["identb"][:, :],
                                                    t["maskq"][:, :], start=False, stop=True)
                            ins.then_inc(q["s_full"], 1)
                        elif kind == "MT":
                            slot, j = e
                            k = sec.add("mt_full")
                            pe.wait_ge(q["mt_full"], k)
                            if sec.get("m_copied"):
                                pe.wait_ge(q["m_copied"], sec.get("m_copied"))
                            if sec.get("y_done"):
                                pe.wait_ge(q["y_done"], sec.get("y_done"))
                            for i in range(TPB):
                                ins = pe.matmul(M[ROWS:SROWS, i * P:(i + 1) * P], mt[:, j % M_SLOTS, i, :],
                                                t["identb"][:, :], start=True, stop=True)
                            ins.then_inc(q["m_split"], 1)
                            mrow[e] = sec.add("m_copied")
                        elif kind == "ST":
                            s, slot, j, k = e
                            if k == 0 and (slot, j) in mrow and not (slot == 0 and j < LEAD):
                                pe.wait_ge(q["m_copied"], mrow[(slot, j)])
                            if s >= ST_SLOTS:
                                pe.wait_ge(q["exp_done"], s - ST_SLOTS + 1)
                            c0 = max(0, k - TPB * j) * P
                            diag = k >= TPB * j
                            q0 = j * BW
                            ins = pe.matmul(ST[s % ST_SLOTS][:, c0:BW], kst[slot][0:SROWS, k * P:(k + 1) * P],
                                            qst[slot][0:SROWS, q0 + c0:q0 + BW], start=True, stop=not diag)
                            if diag:
                                ins = pe.matmul(ST[s % ST_SLOTS][:, c0:c0 + P], t["identb"][:, :], t["maskk"][:, :],
                                                start=False, stop=True)
                            ins.then_inc(q["st_full"], 1)
                            sec.add("exp_done")
                        elif kind == "PV":
                            g, slot, j, G = e
                            pe.wait_ge(q["exp_done"], TPB * (g + 1))
                            if G == 0:
                                if outs:
                                    pe.wait_ge(q["od_done"], outs)
                                if j == 0 and slot == 1:
                                    sec.add("v_full")
                                    pe.wait_ge(q["v_full"], 1)
                            for r in range(TPB):
                                k = TPB * G + r
                                c0 = r * P if G == j else 0
                                row = 32 * r if j else 0
                                ins = pe.matmul(O[row:row + 32, c0:BW], vpad[slot][:, k, :],
                                                prob[:, (4 * g + r) % NP, c0:BW],
                                                start=(G == 0 if j else r == 0),
                                                stop=(G == j if j else r == 3), tile_position=(0, row),
                                                skip_group_check=True)
                            ins.then_inc(q["pv_done"], 1)
                            if G == j:
                                outs += 1
                                sec.add("od_done")
                        elif kind == "YO":
                            slot, j = e
                            groups += 1
                            pe.wait_ge(q["od_done"], groups)
                            if sec.get("m_copied"):
                                pe.wait_ge(q["m_copied"], sec.get("m_copied"))
                            if sec.get("y_done"):
                                pe.wait_ge(q["y_done"], sec.get("y_done"))
                            rows = P if j else 32
                            for i in range(TPB):
                                ins = pe.matmul(M[:, 32 * i:32 * i + 32], od[0:rows, j % 2, i * P:(i + 1) * P],
                                                t["sel"][0:rows, :], start=True, stop=True)
                            ins.then_inc(q["y_full"], 1)
                            sec.add("y_done")
                        elif kind == "V" and e == 0:
                            sec.add("v_next")
                    if sec.get("v_next"):
                        sec.add("v_full")
                    settle(pe, sec, ("s_read", "s_last_read", "mt_full", "m_copied", "exp_done", "od_done",
                                     "y_done", "v_full", "stack0", "stack1"))

                section("first")
                with pe.Fori(0, H // 2):
                    section("body")

            @block.scalar
            def _(act):
                def vcopy(slot, head):
                    act.activation(vpad[slot][:, :, 0:C], t["v"][:, :, bass.ds(head * C, C)],
                                   ACT.Copy).then_inc(q["v_full"], 1)

                def section(name, h):
                    sec = Section()
                    if name == "first":
                        vcopy(0, 0)
                    outs = 0
                    for kind, e in sections[name]:
                        if kind == "MT":
                            slot, j = e
                            act.wait_ge(q["m_split"], sec.add("m_split"))
                            act.activation(qst[slot][ROWS:SROWS, j * BW:(j + 1) * BW], M[ROWS:SROWS, :],
                                           ACT.Copy).then_inc(q["m_copied"], 1)
                        elif kind == "ST":
                            s, slot, j, k = e
                            act.wait_ge(q["st_full"], sec.add("st_full"))
                            if s % TPB == 0 and s >= NP:
                                act.wait_ge(q["pv_done"], s // 4 - 1)
                            c0 = max(0, k - TPB * j) * P
                            act.activation(prob[:, s % NP, c0:BW], ST[s % ST_SLOTS][:, c0:BW],
                                           ACT.Exp).then_inc(q["exp_done"], 1)
                        elif kind == "PV":
                            sec.add("pv_done")
                        elif kind == "OD":
                            slot, j = e
                            act.wait_ge(q["pv_done"], sec.get("pv_done"))
                            rows = P if j else 32
                            act.activation(od[0:rows, j % 2, :], O[0:rows, :], ACT.Copy).then_inc(q["od_done"], 1)
                        elif kind == "V":
                            vcopy(e, h + (1 if e else 2))
                        elif kind == "FREE":
                            act.activation(tok[:, 0:1], t["mod"][0:1, 0:1], ACT.Copy).then_inc(q["heads_free"], 1)
                    settle(act, sec, ("m_split", "st_full", "pv_done"))

                section("first", 0)
                with act.Fori(0, H // 2) as pair:
                    h = pair * 2
                    section("body", h)

            @block.vector
            def _(dve):
                def section(name, h):
                    sec = Section()
                    for kind, e in sections[name]:
                        if kind == "S":
                            n, (slot, j, r, c, k0, k1), last = e
                            dve.wait_ge(q["s_full"], sec.add("s_full"))
                            ins = dve.tensor_reduce(mx[:, j % M_SLOTS, r, c:c + 1], S[n % S_SLOTS][:, 0:k1 - k0], AX_X, ALU.max)
                            if not last:
                                ins.then_inc(q["s_read"], 1)
                                continue
                            ins.then_inc(q["dve_chain"], 1)
                            dve.wait_ge(q["dve_chain"], sec.add("dve_chain"))
                            dve.tensor_reduce(mq[:, j % M_SLOTS, :], mx[:, j % M_SLOTS, :, 0:c + 1], AX_X,
                                              ALU.max).then_inc(q["m_full"], 1)
                        elif kind == "YO":
                            slot, j = e
                            dve.wait_ge(q["y_full"], sec.add("y_full"))
                            y = M[:, 0:32 * TPB].rearrange("p (a c) -> p a c", c=32)
                            dve.reciprocal(rl[:, j % 2, :], y[:, :, C]).then_inc(q["y_chain"], 1)
                            dve.wait_ge(q["y_chain"], sec.add("y_chain"))
                            dve.tensor_tensor(
                                t["y"][:, TPB * j:TPB * j + TPB, bass.ds((h + slot) * C, C)], y[:, :, 0:C],
                                rl[:, j % 2, :].unsqueeze(2).broadcast_to([P, TPB, C]),
                                ALU.mult).then_inc(q["y_done"], 1)
                    settle(dve, sec, ("s_full", "dve_chain", "y_full", "y_chain"))

                section("first", 0)
                with dve.Fori(0, H // 2) as pair:
                    h = pair * 2
                    section("body", h)

            @block.gpsimd
            def _(pool):
                def section(name):
                    sec = Section()
                    for kind, e in sections[name]:
                        if kind == "S" and e[2]:
                            j = e[1][1] % M_SLOTS
                            pool.wait_ge(q["m_full"], sec.add("m_full"))
                            pool.tensor_scalar(nm[:, j, :], mq[:, j, :], -1.0, None,
                                               ALU.mult).then_inc(q["s_last_read"], 1)
                            pool.tensor_scalar(mt[:, j, :, 0], mq[:, j, :], -1.0, None,
                                               ALU.mult).then_inc(q["pool_chain"], 1)
                            pool.wait_ge(q["pool_chain"], sec.add("pool_chain"))
                            pool.tensor_tensor(mt[:, j, :, 1], nm[:, j, :], mt[:, j, :, 0],
                                               ALU.subtract).then_inc(q["mt_full"], 1)
                    settle(pool, sec, ("m_full", "pool_chain"))

                section("first")
                with pool.Fori(0, H // 2):
                    section("body")


def project(nc, t, d):
    with ExitStack() as ctx:
        def sb(name, shape, dt):
            return ctx.enter_context(nc.sbuf_tensor(name, shape, dt))

        def sem(name):
            return ctx.enter_context(nc.semaphore(name))

        WR = 2
        wraw = sb("wraw", [P, WR, WU], F32)
        wu = sb("wu", [P, NS, D], F32)
        gwT = sb("gwT", [P, NS, E], F32)
        bias = sb("bias", [P, E], F32)
        yT = sb("yT", [P, NS, BW], F32)
        xn = sb("xn2", [P, TPB, D], F32)
        stats = sb("stats2", [P, TPB, 6], F32)
        mv = sb("mv2", [P, TPB, 2], F32)
        ve = sb("ve2", [P, TPB], F32)
        rstd = sb("rstd2", [P, TPB], F32)
        half = sb("half2", [P, TPB], F32)
        sc = sb("sc", [P, NT, E], F32)
        sfc = sb("sfc", [P, NT, E], F32)
        ge, rank = (xn[:, 2 * i:2 * i + 2, :].rearrange("p a (b e) -> p (a b) e", e=E) for i in range(2))
        cwe = sfc[:, :, :].rearrange("p t e -> p (t e)")
        gs = sb("gs", [P, NT, NG], F32)
        grank = sb("grank", [P, NT, NG], F32)
        gtmp = sb("gtmp2", [P, NT, NG], F32)
        wsum = sb("wsum", [P, NT], F32)
        cwT = sb("cwT", [P, 4, P], F32)
        tpy = [ctx.enter_context(nc.psum_tensor(f"tpy{i}", [P, BW], F32)) for i in range(2)]
        pj = [ctx.enter_context(nc.psum_tensor(f"pj{i}", [P, BW], F32)) for i in range(2)]
        tpx = [ctx.enter_context(nc.psum_tensor(f"tpx{i}", [P, BW], F32)) for i in range(2)]
        gl = ctx.enter_context(nc.psum_tensor("gl", [P, NT * E], F32))
        tpc = ctx.enter_context(nc.psum_tensor("tpc", [P, 4 * P], F32))

        s_w = [sem(f"wraw_in{i}") for i in range(WR)]
        s_wu, s_gw, s_bias, s_x1, s_cwo = sem("wu_in"), sem("gw_in"), sem("bias_in"), sem("x1_out"), sem("cw_out")
        s_pool, s_dve, s_cut, s_half = sem("pool_chain2"), sem("dve_chain2"), sem("cut"), sem("half_ready")
        s_tpy, s_yT, s_wus, s_pj, s_x1r = sem("tpy"), sem("yT_ready"), sem("wu_scaled"), sem("pj"), sem("x1_ready")
        s_ve, s_rstd, s_xn, s_tpx, s_h2 = sem("ve_ready"), sem("rstd_ready"), sem("xn_ready"), sem("tpx"), sem("h2_ready")
        s_gl, s_sig, s_cw, s_tpc, s_cwT = sem("gl"), sem("sigmoid"), sem("cw_ready"), sem("tpc"), sem("cwT_ready")
        whi, wlo = t["whi"], t["wlo"]

        with nc.Block() as block:
            @block.sync
            def _(sp):
                for u in range(U):
                    if u >= WR:
                        sp.wait_ge(s_cut, u - WR + 1)
                    sp.dma_start(wraw[:, u % WR, :], d["wcat"][u]).then_inc(s_w[u % WR], 16)

            @block.scalar
            def _(act):
                act.dma_start(wu[:, :, :], d["WuT"].rearrange("(s p) n -> p s n", p=P)).then_inc(s_wu, 16)
                act.dma_start(gwT[:, :, :], d["gwT"].rearrange("(s p) n -> p s n", p=P)).then_inc(s_gw, 16)
                act.dma_start(bias[:, :], d["gbias"].unsqueeze(0).broadcast_to([P, E])).then_inc(s_bias, 16)

                def turned(b):
                    if b >= 1:
                        act.wait_ge(s_pj, 2 * b)
                    for s in range(NS):
                        act.wait_ge(s_tpy, NS * b + s + 1)
                        act.activation(yT[:, s, :], tpy[s][:, :], ACT.Copy).then_inc(s_yT, 1)

                turned(0)
                for b in range(NB):
                    if b + 1 < NB:
                        turned(b + 1)
                    for s in range(NS):
                        act.wait_ge(s_tpx, NS * b + s + 1)
                        act.activation(t["h2"][:, b, s, :], tpx[s][:, :], ACT.Identity,
                                       scale=t["mod"][:, 8 + s:9 + s],
                                       bias=t["mod"][:, 6 + s:7 + s]).then_inc(s_h2, 1)
                    act.wait_ge(s_x1r, 2 * (b + 1))
                    act.dma_start(d["x1"][b], t["x"][:, TPB * b:TPB * b + TPB, :].rearrange(
                        "p a n -> p (a n)")).then_inc(s_x1, 16)
                act.wait_ge(s_gl, 1)
                act.activation(sc[:, :, :], gl[:, :].rearrange("p (a n) -> p a n", n=E),
                               ACT.Sigmoid).then_inc(s_sig, 1)
                act.wait_ge(s_tpc, 1)
                act.activation(cwT[:, :, :], tpc[:, :].rearrange("p (a n) -> p a n", a=4), ACT.Copy).then_inc(s_cwT, 1)
                act.wait_ge(s_cwT, 1)
                for g in range(4):
                    dst = d["cw"][g].rearrange("e (a k) -> (e a) k", k=P)
                    act.dma_start(dst, cwT[:, g, :]).then_inc(s_cwo, 16)
                act.wait_ge(s_x1, 16 * NB)
                act.wait_ge(s_cwo, 64)

            @block.gpsimd
            def _(pool):
                pool.memset(half[:, :], -0.5).then_inc(s_half, 1)
                pool.wait_ge(s_half, 1)
                n = 0
                for u in range(U):
                    if u % 2 == 0 and u // 2 < NB:
                        pool.wait_ge(s_ve, u // 2 + 1)
                        pool.tensor_tensor(rstd[:, :], ve[:, :], half[:, :], ALU.pow).then_inc(s_rstd, 1)
                    pool.wait_ge(s_w[u % WR], 16 * (u // WR + 1))
                    pool.tensor_copy(whi[:, u, :], wraw[:, u % WR, :]).then_inc(s_pool, 1)
                    n += 1
                    pool.wait_ge(s_pool, n)
                    pool.tensor_tensor(wlo[:, u, :], wraw[:, u % WR, :], whi[:, u, :], ALU.subtract).then_inc(s_cut, 1)

            @block.vector
            def _(dve):
                n = [0]

                def link(ins):
                    n[0] += 1
                    ins.then_inc(s_dve, 1)
                    dve.wait_ge(s_dve, n[0])

                dve.wait_ge(s_wu, 16)
                for s in range(NS):
                    dve.tensor_tensor(wu[:, s, :], wu[:, s, :], t["gab"][:, 0:D], ALU.mult).then_inc(s_wus, 1)
                for b in range(NB):
                    for i in range(2):
                        dve.wait_ge(s_pj, 2 * b + i + 1)
                        x = t["x"][:, TPB * b + 2 * i:TPB * b + 2 * i + 2, :]
                        dve.tensor_tensor(x, x, pj[i][:, :].rearrange("p (a n) -> p a n", a=2),
                                          ALU.add).then_inc(s_x1r, 1)
                    dve.wait_ge(s_x1r, 2 * b + 2)
                    for i in range(TPB):
                        ins = dve.bn_stats(stats[:, i, :], t["x"][:, TPB * b + i, :])
                    link(ins)
                    for i in range(TPB):
                        ins = dve.bn_aggr(mv[:, i, :], stats[:, i, :])
                    link(ins)
                    dve.tensor_scalar(ve[:, :], mv[:, :, 1], EPS, None, ALU.add).then_inc(s_ve, 1)
                    dve.wait_ge(s_rstd, b + 1)
                    dve.wait_ge(s_tpx, NS * b)
                    for i in range(TPB):
                        dve.tensor_scalar(xn[:, i, :], t["x"][:, TPB * b + i, :], mv[:, i, 0:1],
                                          rstd[:, i:i + 1], ALU.subtract, ALU.mult).then_inc(s_xn, 1)
                dve.wait_ge(s_sig, 1)
                dve.wait_ge(s_bias, 16)
                link(dve.tensor_tensor(sfc[:, :, :], sc[:, :, :], bias[:, :].unsqueeze(1).broadcast_to([P, NT, E]),
                                       ALU.add))
                g4 = sfc[:, :, :].rearrange("p t (g k) -> p t g k", k=E // NG)
                pairs = [(a, b) for a in range(4) for b in range(a + 1, 4)]
                for m, (a, b) in enumerate(pairs):
                    dst = gtmp if m else gs
                    link(dve.tensor_tensor(dst[:, :, :], g4[:, :, :, a], g4[:, :, :, b], ALU.add))
                    if m:
                        link(dve.tensor_tensor(gs[:, :, :], gs[:, :, :], gtmp[:, :, :], ALU.max))

                def ranks(rank, val, tmp, n):
                    for i in range(n):
                        ins = dve.memset(rank[:, :, i:i + 1], float(n - 1 - i))
                    link(ins)
                    for k in range(1, n):
                        link(dve.tensor_tensor(tmp[:, :, 0:n - k], val[:, :, 0:n - k], val[:, :, k:n], ALU.is_ge))
                        link(dve.tensor_tensor(rank[:, :, k:n], rank[:, :, k:n], tmp[:, :, 0:n - k], ALU.add))
                        link(dve.tensor_tensor(rank[:, :, 0:n - k], rank[:, :, 0:n - k], tmp[:, :, 0:n - k],
                                               ALU.subtract))

                ranks(grank, gs, gtmp, NG)
                link(dve.tensor_scalar(gtmp[:, :, :], grank[:, :, :], float(TG) - 0.5, None, ALU.is_lt))
                keep = gtmp[:, :, :].unsqueeze(3).broadcast_to([P, NT, NG, E // NG])
                link(dve.tensor_tensor(g4, g4, keep, ALU.mult))
                link(dve.tensor_scalar(gtmp[:, :, :], gtmp[:, :, :], -1.0, 1e30, ALU.add, ALU.mult))
                link(dve.tensor_tensor(g4, g4, keep, ALU.add))
                ranks(rank, sfc, ge, E)
                link(dve.tensor_scalar(rank[:, :, :], rank[:, :, :], float(TOPK) - 0.5, None, ALU.is_lt))
                link(dve.tensor_tensor(sc[:, :, :], sc[:, :, :], rank[:, :, :], ALU.mult))
                link(dve.tensor_reduce(wsum[:, :], sc[:, :, :], AX_X, ALU.add))
                link(dve.tensor_scalar(wsum[:, :], wsum[:, :], 1e-20, None, ALU.add))
                link(dve.reciprocal(wsum[:, :], wsum[:, :]))
                link(dve.tensor_scalar(wsum[:, :], wsum[:, :], RSCALE, None, ALU.mult))
                split = sc[:, :, :].rearrange("p (g a) e -> p g a e", g=4)
                w4 = wsum[:, :].rearrange("p (g a) -> p g a", g=4)
                for g in range(4):
                    ins = dve.tensor_tensor(cwe[:, g * P:(g + 1) * P].rearrange("p (e a) -> p a e", e=E),
                                            split[:, g, :, :], w4[:, g, :].unsqueeze(2).broadcast_to([P, 8, E]),
                                            ALU.mult)
                ins.then_inc(s_cw, 1)

            @block.tensor
            def _(pe):
                def turn(b):
                    for s in range(NS):
                        if b >= 1:
                            pe.wait_ge(s_yT, NS * (b - 1) + s + 1)
                        for i in range(TPB):
                            ins = pe.transpose(tpy[s][:, i * P:(i + 1) * P],
                                               t["y"][:, TPB * b + i, s * P:(s + 1) * P], t["identf"][:, :])
                        ins.then_inc(s_tpy, 1)

                def proj(b):
                    pe.wait_ge(s_yT, NS * (b + 1))
                    for i in range(TPB):
                        if b >= 1 and i % 2 == 0:
                            pe.wait_ge(s_x1r, 2 * (b - 1) + i // 2 + 1)
                        for s in range(NS):
                            ins = pe.matmul(pj[i // 2][:, (i % 2) * D:(i % 2 + 1) * D],
                                            yT[:, s, i * P:(i + 1) * P], wu[:, s, :],
                                            start=(s == 0), stop=(s == NS - 1))
                        if i % 2:
                            ins.then_inc(s_pj, 1)

                def normed(b):
                    pe.wait_ge(s_xn, TPB * (b + 1))
                    for s in range(NS):
                        if b >= 1:
                            pe.wait_ge(s_h2, NS * (b - 1) + s + 1)
                        for i in range(TPB):
                            ins = pe.transpose(tpx[s][:, i * P:(i + 1) * P], xn[:, i, s * P:(s + 1) * P],
                                               t["identf"][:, :])
                        ins.then_inc(s_tpx, 1)

                def logits(b):
                    pe.wait_ge(s_h2, NS * (b + 1))
                    for i in range(TPB * b, TPB * b + TPB):
                        for s in range(NS):
                            ins = pe.matmul(gl[:, i * E:(i + 1) * E], t["h2"][:, b, s, (i - TPB * b) * P:(i - TPB * b + 1) * P], gwT[:, s, :],
                                            start=(s == 0), stop=(s == NS - 1))
                    return ins

                turn(0)
                pe.wait_ge(s_wus, NS)
                turn(1)
                proj(0)
                pe.wait_ge(s_gw, 16)
                for b in range(NB):
                    if b + 2 < NB:
                        turn(b + 2)
                    if b + 1 < NB:
                        proj(b + 1)
                    normed(b)
                    if b >= 1:
                        logits(b - 1)
                logits(NB - 1).then_inc(s_gl, 1)
                pe.wait_ge(s_cw, 1)
                for g in range(4):
                    ins = pe.transpose(tpc[:, g * P:(g + 1) * P],
                                       cwe[:, g * P:(g + 1) * P], t["identf"][:, :])
                ins.then_inc(s_tpc, 1)


def experts(nc, t, d):
    with ExitStack() as ctx:
        def sb(name, shape, dt):
            return ctx.enter_context(nc.sbuf_tensor(name, shape, dt))

        whi, wlo, h2 = t["whi"], t["wlo"], t["h2"]
        HC = E // 4
        hhi = sb("hhi", [P, 2, NS, BW], F32R)
        hlo = sb("hlo", [P, 2, NS, BW], F32R)
        cwb = sb("cwb", [P, 2 * HC, BW], F32)
        sg = sb("sg", [P, 2, BW], F32)
        pr = sb("pr", [P, 2, BW], F32)
        ahi = sb("ahi", [P, 2, BW], F32R)
        alo = sb("alo", [P, 2, BW], F32R)
        x1 = sb("x1b", [P, 2, TPB * D], F32)
        tok = sb("tok4", [1, 2], F32)
        hg = [ctx.enter_context(nc.psum_tensor(f"hg{i}", [P, BW], F32)) for i in range(2)]
        hu = [ctx.enter_context(nc.psum_tensor(f"hu{i}", [P, BW], F32)) for i in range(2)]
        ya = [ctx.enter_context(nc.psum_tensor(f"ya{i}", [P, NS, BW], F32)) for i in range(2)]
        names = ("h_full", "h_free", "gu_full", "silu", "dve_chain", "pr_full", "ahi_done", "act_full", "y_full",
                 "z_add", "z_full", "zt_full", "out_full", "cw_free", "x1_in0", "x1_in1", "cw_in0", "cw_in1",
                 "out_done0", "out_done1")
        q = {n: ctx.enter_context(nc.semaphore("ex_" + n)) for n in names}
        z = sb("z", [P, NS, BW], F32)

        def settle(eng, counts):
            for n, c in counts:
                eng.wait_ge(q[n], c)
            eng.drain()
            for n, c in counts:
                eng.nop().then_inc(q[n], -c)

        seq = [(p, u) for p in range(2) for u in range(U)]
        NQ = len(seq)

        with nc.Block() as block:
            @block.sync
            def _(sp):
                sp.sem_inc(q["cw_free"], 2)
                with sp.Fori(0, NB // 2) as pair:
                    b = pair * 2
                    for p in range(2):
                        sp.dma_start(x1[:, p, :], d["x1"][bass.ds(b + p, 1), :, :].rearrange("a p n -> (a p) n")
                                     ).then_inc(q[f"x1_in{p}"], 16)
                        for k in range(4):
                            sp.wait_ge(q["cw_free"], 4 * p + k + 1)
                            src = d["cw"][bass.ds(pair, 1), k * HC:(k + 1) * HC, p * BW:(p + 1) * BW]
                            sp.dma_start(cwb[:, k % 2 * HC:(k % 2 + 1) * HC, :], src.broadcast_to([P, HC, BW])
                                         ).then_inc(q[f"cw_in{k % 2}"], 16)
                    for p in range(2):
                        sp.wait_ge(q["out_full"], p + 1)
                        dst = d["out"][bass.ds((b + p) * TPB, TPB), :, :].rearrange("a p n -> p a n")
                        sp.dma_start(dst, x1[:, p, :].rearrange("p (a n) -> p a n", a=TPB)
                                     ).then_inc(q[f"out_done{p}"], 16)
                    for p in range(2):
                        sp.wait_ge(q[f"out_done{p}"], 16)
                    sp.drain()
                    for n, c in (("cw_free", 8), ("out_full", 2), ("out_done0", 16), ("out_done1", 16)):
                        sp.nop().then_inc(q[n], -c)

            @block.gpsimd
            def _(pool):
                pool.sem_inc(q["h_free"], 2)
                with pool.Fori(0, NB // 2) as pair:
                    b = pair * 2
                    for p in range(2):
                        pool.wait_ge(q["h_free"], p + 1)
                        src = h2[:, bass.ds(b + p, 1), :, :].rearrange("p a s n -> p (a s) n")
                        pool.tensor_copy(hhi[:, p, :, :], src).then_inc(q["h_full"], 1)
                        pool.drain()
                        pool.tensor_tensor(hlo[:, p, :, :], src, hhi[:, p, :, :], ALU.subtract).then_inc(q["h_full"], 1)
                    pool.drain()
                    pool.nop().then_inc(q["h_free"], -2)

            @block.tensor
            def _(pe):
                def up(n):
                    p, u = seq[n]
                    if u == 0:
                        pe.wait_ge(q["h_full"], 2 * p + 2)
                    for k, bank in ((0, hg[n % 2]), (1, hu[n % 2])):
                        m = 0
                        for s in range(NS):
                            c0 = (k * NS + s) * I
                            for w, h in ((whi, hhi), (whi, hlo), (wlo, hhi)):
                                ins = pe.matmul(bank[:, :], w[:, u, c0:c0 + I], h[:, p, s, :],
                                                start=(m == 0), stop=(m == 5))
                                m += 1
                    ins.then_inc(q["gu_full"], 1)

                def down(n):
                    p, u = seq[n]
                    pe.wait_ge(q["act_full"], n + 1)
                    for s in range(NS):
                        c0 = 2 * NS * I + s * P
                        for m, (w, a) in enumerate(((whi, ahi), (whi, alo), (wlo, ahi))):
                            ins = pe.matmul(ya[p][:, s, :], w[:, u, c0:c0 + P], a[:, n % 2, :],
                                            start=(u == 0 and m == 0), stop=(u == U - 1 and m == 2))
                    if u == U - 1:
                        ins.then_inc(q["y_full"], 1)

                def back(p):
                    pe.wait_ge(q["z_full"], 2 * p + 2)
                    out = ya[p][:, :, :].rearrange("p s (i n) -> p (s i) n", n=D)
                    for i in range(TPB):
                        for s in range(NS):
                            ins = pe.transpose(out[:, i, s * P:(s + 1) * P], z[:, s, i * P:(i + 1) * P],
                                               t["identf"][:, :])
                    ins.then_inc(q["zt_full"], 1)

                with pe.Fori(0, NB // 2):
                    for n in range(NQ):
                        up(n)
                        if n >= 1:
                            down(n - 1)
                        if n == U + 2:
                            back(0)
                    down(NQ - 1)
                    back(1)
                    settle(pe, (("h_full", 4), ("act_full", NQ), ("z_full", 4)))

            @block.scalar
            def _(act):
                def scaled(p):
                    for s in range(NS):
                        act.wait_ge(q["z_add"], 2 * p + s + 1)
                        act.activation(z[:, s, :], z[:, s, :], ACT.Copy, scale=t["gb"][:, s:s + 1]
                                       ).then_inc(q["z_full"], 1)

                def token(name):
                    act.activation(tok[:, 0:1], t["mod"][0:1, 0:1], ACT.Copy).then_inc(q[name], 1)

                def high(n):
                    act.wait_ge(q["pr_full"], n + 1)
                    act.activation(ahi[:, n % 2, :], pr[:, n % 2, :], ACT.Copy).then_inc(q["ahi_done"], 1)
                    if seq[n][1] < E and seq[n][1] % HC == HC - 1:
                        token("cw_free")

                with act.Fori(0, NB // 2):
                    for n in range(NQ):
                        act.wait_ge(q["gu_full"], n + 1)
                        act.activation(sg[:, n % 2, :], hg[n % 2][:, :], ACT.Silu).then_inc(q["silu"], 1)
                        if seq[n][1] == U - 1:
                            token("h_free")
                        high(n)
                        if n == U + 1:
                            scaled(0)
                    scaled(1)
                    settle(act, (("gu_full", NQ), ("pr_full", NQ), ("z_add", 4)))

            @block.vector
            def _(dve):
                with dve.Fori(0, NB // 2) as pair:
                    b = pair * 2
                    chain = [0]

                    def summed(p):
                        dve.wait_ge(q["y_full"], p + 1)
                        for s in range(NS):
                            dve.tensor_tensor(z[:, s, :], ya[p][:, s, :],
                                              h2[:, bass.ds(b + p, 1), s, :].rearrange("p a n -> p (a n)"), ALU.add).then_inc(q["z_add"], 1)

                    def result(p):
                        dve.wait_ge(q["zt_full"], p + 1)
                        dve.wait_ge(q[f"x1_in{p}"], 16)
                        dve.tensor_tensor(x1[:, p, :], x1[:, p, :], ya[p][:, :, :].rearrange("p s n -> p (s n)"),
                                          ALU.add).then_inc(q["out_full"], 1)

                    for n in range(NQ):
                        p, u = seq[n]
                        dve.wait_ge(q["silu"], n + 1)
                        if u < E:
                            dve.tensor_tensor(sg[:, n % 2, :], sg[:, n % 2, :], hu[n % 2][:, :],
                                              ALU.mult).then_inc(q["dve_chain"], 1)
                            chain[0] += 1
                            dve.wait_ge(q["dve_chain"], chain[0])
                            if u % HC == 0:
                                dve.wait_ge(q[f"cw_in{u // HC % 2}"], 16 * (2 * p + u // HC // 2 + 1))
                            dve.tensor_tensor(pr[:, n % 2, :], sg[:, n % 2, :], cwb[:, u % (2 * HC), :],
                                              ALU.mult).then_inc(q["pr_full"], 1)
                        else:
                            dve.tensor_tensor(pr[:, n % 2, :], sg[:, n % 2, :], hu[n % 2][:, :],
                                              ALU.mult).then_inc(q["pr_full"], 1)
                        dve.wait_ge(q["ahi_done"], n + 1)
                        dve.tensor_tensor(alo[:, n % 2, :], pr[:, n % 2, :], ahi[:, n % 2, :],
                                          ALU.subtract).then_inc(q["act_full"], 1)
                        if n == U:
                            summed(0)
                        if n == U + 4:
                            result(0)
                    summed(1)
                    result(1)
                    settle(dve, (("silu", NQ), ("dve_chain", chain[0]), ("ahi_done", NQ), ("y_full", 2),
                                 ("zt_full", 2), ("cw_in0", 64), ("cw_in1", 64), ("x1_in0", 16), ("x1_in1", 16)))


def build(nc, d):
    with ExitStack() as ctx:
        def sb(c, name, shape, dt):
            return c.enter_context(nc.sbuf_tensor(name, shape, dt))

        t = {}
        t["identf"] = sb(ctx, "identf", [P, P], F32)
        t["mod"] = sb(ctx, "mod", [P, 12], F32)
        t["gb"] = sb(ctx, "gb", [P, NS], F32)
        t["h2"] = sb(ctx, "h2", [P, NB, NS, BW], F32)
        t["y"] = t["h2"][:, :, :, :].rearrange("p b s n -> p (b s n)").rearrange("p (i n) -> p i n", n=D)
        with ExitStack() as mid:
            t["gab"] = sb(mid, "gab", [P, 2 * D], F32)
            t["x"] = sb(mid, "xres", [P, NT, D], F32)
            with ExitStack() as early:
                t["identb"] = sb(early, "identb", [P, P], BF16)
                t["maskq"] = sb(early, "maskq", [P, P], BF16)
                t["maskk"] = sb(early, "maskk", [P, P], BF16)
                t["sel"] = sb(early, "sel", [P, 32], F32)
                t["v"] = sb(early, "v", [P, NT, HPAD * C], F32)
                t["vpad"] = [sb(early, f"vpad{i}", [P, NT, 32], F32) for i in range(2)]
                t["qst"] = [sb(early, f"qst{i}", [P, T], BF16) for i in range(2)]
                t["kst"] = [sb(early, f"kst{i}", [P, T], BF16) for i in range(2)]
                prepare(nc, t, d)
                attend(nc, t, d)
            for name in ("whi", "wlo"):
                t[name] = ctx.enter_context(nc.sbuf_tensor(name, [P, U, WU], F32R, side="right"))
            project(nc, t, d)
        experts(nc, t, d)


_OUT = ((1, T, D), "float32")


def kernel(**inputs):
    import numpy as _np
    import concourse.bacc as _bacc
    from concourse.bass_utils import run_bass_kernel_spmd as _run

    a = {k: _np.asarray(v) for k, v in inputs.items()}

    def units(w, s):
        both = _np.concatenate([w, s.reshape(2, I, D)], axis=0)
        return both.transpose(0, 2, 1).reshape(U, NS, P, I).transpose(0, 2, 1, 3).reshape(U, P, NS * I)

    down = _np.concatenate([a["L0_ffn_Wd"].transpose(0, 2, 1), a["L0_ffn_Ws_d"].T.reshape(2, I, D)], axis=0)
    arrays = {
        "x": a["L0_attn_x"], "c": a["L0_c"], "wmod": a["L0_wmod"], "bu": a["L0_attn_bu"],
        "WqT": a["L0_attn_Wq"].T, "WkT": a["L0_attn_Wk"].T, "WvT": a["L0_attn_Wv"].T,
        "WuT": a["L0_attn_Wu"].T, "gwT": a["L0_ffn_gate_w"].T, "gbias": a["L0_ffn_gate_bias"],
        "wcat": _np.concatenate([units(a["L0_ffn_Wg"], a["L0_ffn_Ws_g"]),
                                 units(a["L0_ffn_Wu"], a["L0_ffn_Ws_u"]), down], axis=2),
    }
    arrays = {f"in_{k}": _np.ascontiguousarray(v) for k, v in arrays.items()}
    nc = _bacc.Bacc("TRN2", target_bir_lowering=False, num_devices=1)
    d = {k[3:]: nc.dram_tensor(k, v.shape, mybir.dt.from_np(v.dtype), kind="ExternalInput").ap()
         for k, v in arrays.items()}
    for name in ("qs", "ks"):
        d[name] = nc.dram_tensor(name, [3, HPAD * C, T], BF16).ap()
    d["x1"] = nc.dram_tensor("x1", [NB, P, TPB * D], F32).ap()
    d["cw"] = nc.dram_tensor("cw", [NB // 2, E, 2 * BW], F32).ap()
    out = nc.dram_tensor("out_0", _OUT[0], mybir.dt.from_np(_np.dtype(_OUT[1])), kind="ExternalOutput").ap()
    d["out"] = out.rearrange("a (n p) c -> (a n) p c", p=P)
    build(nc, d)
    r = _run(nc, [arrays], core_ids=[0])
    return r.results[0]["out_0"]
```

```python
from contextlib import ExitStack

import concourse.bass as bass
from concourse import mybir

F32 = mybir.dt.float32
F32R = mybir.dt.float32r
BF16 = mybir.dt.bfloat16
ALU = mybir.AluOpType
ACT = mybir.ActivationFunctionType
AX_X = mybir.AxisListType.X

P = 128
T = 4096
D = 256
H = 16
C = D // H
NS = D // P
NT = T // P
BW = 512
NB = T // BW
TPB = BW // P
EPS = 1e-5
MASKED = -1e30
FLOOR = 0.25
HPAD = H + 1

QPARTS = (0, 0, 0, 1, 1, 2)
KPARTS = (0, 1, 2, 0, 1, 0)
ROWS = C * len(QPARTS)
SROWS = ROWS + 2

E = 16
TOPK = 4
NG = 4
TG = 2
RSCALE = 2.5
I = 128
U = E + 2
WU = 2 * NS * I + D

LEAD = 5
SW = 1
S_SLOTS = 3
ST_SLOTS = 3
M_SLOTS = 4


def prepare(nc, t, d):
    with ExitStack() as ctx:
        def sb(name, shape, dt):
            return ctx.enter_context(nc.sbuf_tensor(name, shape, dt))

        def sem(name):
            return ctx.enter_context(nc.semaphore(name))

        QKR = 4
        wmod = sb("wmod", [P, NS, 6 * D], F32)
        ccol = sb("ccol", [P, NS], F32)
        scol = sb("scol", [P, NS], F32)
        wrep = sb("wrep", [P, 3, C], F32)
        onb = sb("onb", [P, P // C, C], F32)
        wbd = t["wbd"]
        hT = t["h2"]
        xn = sb("xn", [P, 2, TPB, D], F32)
        stats = sb("stats", [P, NT, 6], F32)
        mv = sb("mv", [P, NT, 2], F32)
        ve = sb("ve", [P, NT], F32)
        rstd = sb("rstd", [P, NT], F32)
        half = sb("half", [P, NT], F32)
        grow = sb("grow", [1, 2 * D], F32)
        gtmp = sb("gtmp", [1, 3, D], F32)
        burow = sb("burow", [1, D], F32)
        gbt = sb("gbt", [P, 3, NS], F32)
        ones1 = sb("ones1", [1, P], F32)
        parts = sb("parts", [P, QKR, 3, BW], BF16)
        rest = sb("rest", [P, QKR, BW], F32)
        tp = [ctx.enter_context(nc.psum_tensor(f"tp{i}", [P, BW], F32)) for i in range(2)]
        qk = [ctx.enter_context(nc.psum_tensor(f"qk{i}", [P, BW], F32)) for i in range(QKR)]
        modp = ctx.enter_context(nc.psum_tensor("modp", [P, BW], F32))

        s_c, s_wm, s_wr, s_bu = sem("c_in"), sem("wmod_in"), sem("wrep_in"), sem("bu_in")
        s_x = [sem(f"x_in{g}") for g in range(4)]
        s_store = [sem(f"parts_out{i}") for i in range(QKR)]
        s_zero = sem("zero_rows_out")
        s_pool, s_const, s_dve = sem("pool_chain"), sem("constants"), sem("dve_chain")
        s_silu, s_modp, s_mod = sem("silu_c"), sem("mod_psum"), sem("mod_ready")
        s_grow, s_bc, s_ve, s_rstd, s_xn = sem("ga_row"), sem("ga_bcast"), sem("ve"), sem("rstd"), sem("xn")
        s_tp, s_hT, s_wbd = sem("transposed"), sem("hT_ready"), sem("wbd_ready")
        s_qk, s_p1, s_r, s_p2, s_p3 = sem("qk_psum"), sem("part1"), sem("rest"), sem("part2"), sem("part3")
        GT = NT // 4
        chunks = [(b, s, w) for b in range(NB) for s in range(NS) for w in range(2)]

        with nc.Block() as block:
            @block.sync
            def _(sp):
                xv = d["x"].rearrange("a (n p) c -> p (a n) c", p=P)
                sp.dma_start(ccol[:, :], d["c"].rearrange("a (s p) -> p (a s)", p=P),
                             allow_slow_non_contiguous=True).then_inc(s_c, 16)
                sp.dma_start(wmod[:, :, :], d["wmod"].rearrange("(s p) n -> p s n", p=P)).then_inc(s_wm, 16)
                for g in range(4):
                    sp.dma_start(t["x"][:, g * GT:(g + 1) * GT, :], xv[:, g * GT:(g + 1) * GT, :]).then_inc(s_x[g], 16)
                sp.wait_ge(s_const, 1)
                for which in ("qs", "ks"):
                    for k in range(3):
                        sp.dma_start(d[which][k, D:HPAD * C, :], t["qst"][0][0:C, :]).then_inc(s_zero, 16)
                for c, (b, s, w) in enumerate(chunks):
                    sp.wait_ge(s_p3, c + 1)
                    dst = d["ks" if w else "qs"][:, s * P:(s + 1) * P, b * BW:(b + 1) * BW]
                    sp.dma_start(dst.rearrange("k p n -> p k n"), parts[:, c % QKR, :, :]).then_inc(s_store[c % QKR], 16)
                for i in range(QKR):
                    sp.wait_ge(s_store[i], 16 * len(chunks) // QKR)
                sp.wait_ge(s_zero, 96)

            @block.gpsimd
            def _(pool):
                n = [0]

                def link(ins):
                    n[0] += 1
                    ins.then_inc(s_pool, 1)
                    pool.wait_ge(s_pool, n[0])

                link(pool.memset(t["qst"][0][0:C, :], 0.0))
                pool.memset(half[:, :], -0.5).then_inc(s_const, 1)
                link(pool.memset(t["identf"][:, :], 0.0))
                link(pool.affine_select(out=t["identf"][:, :], in_=t["identf"][:, :], compare_op=ALU.not_equal,
                                        fill=1.0, base=0, pattern=[[-1, P]], channel_multiplier=1))
                link(pool.memset(onb[:, :, :], 1.0))
                link(pool.affine_select(out=onb[:, :, :], in_=onb[:, :, :], compare_op=ALU.is_ge, fill=0.0,
                                        base=0, pattern=[[-C, P // C], [0, C]], channel_multiplier=1))
                link(pool.affine_select(out=onb[:, :, :], in_=onb[:, :, :], compare_op=ALU.is_ge, fill=0.0,
                                        base=C - 1, pattern=[[C, P // C], [0, C]], channel_multiplier=-1))
                link(pool.memset(ones1[:, :], 1.0))
                link(pool.memset(t["maskq"][:, :], 0.0))
                link(pool.affine_select(out=t["maskq"][:, :], in_=t["maskq"][:, :], compare_op=ALU.is_ge,
                                        fill=MASKED, base=0, pattern=[[-1, P]], channel_multiplier=1))
                link(pool.memset(t["maskk"][:, :], 0.0))
                link(pool.affine_select(out=t["maskk"][:, :], in_=t["maskk"][:, :], compare_op=ALU.is_ge,
                                        fill=MASKED, base=0, pattern=[[1, P]], channel_multiplier=-1))
                link(pool.memset(t["v"][:, :, D:HPAD * C], 0.0))
                for i in range(2):
                    link(pool.memset(t["vpad"][i][:, :, C:32], 0.0))
                    link(pool.memset(t["vpad"][i][:, :, C:C + 1], 1.0))
                    link(pool.memset(t["kst"][i][ROWS:P, :], 1.0))
                    link(pool.memset(t["qst"][i][ROWS:P, :], 0.0))
                pool.memset(half[:, :], -0.5).then_inc(s_const, 1)
                pool.wait_ge(s_const, 2)

                def power(g):
                    pool.wait_ge(s_ve, g + 1)
                    c0, c1 = g * GT, (g + 1) * GT
                    pool.tensor_tensor(rstd[:, c0:c1], ve[:, c0:c1], half[:, c0:c1], ALU.pow).then_inc(s_rstd, 1)

                power(0)
                power(1)
                for c, (b, s, w) in enumerate(chunks):
                    pool.wait_ge(s_p2, c + 1)
                    i = c % QKR
                    pool.tensor_tensor(parts[:, i, 2, :], rest[:, i, :], parts[:, i, 1, :],
                                       ALU.subtract).then_inc(s_p3, 1)
                    if c % 4 == 3 and b % 2 == 0 and b // 2 + 2 < 4:
                        power(b // 2 + 2)

            @block.vector
            def _(dve):
                n = [0]

                def link(ins):
                    n[0] += 1
                    ins.then_inc(s_dve, 1)
                    dve.wait_ge(s_dve, n[0])

                dve.wait_ge(s_const, 2)
                link(dve.tensor_copy(t["identb"][:, :], t["identf"][:, :]))
                link(dve.tensor_tensor(t["sel"][:, :], t["identf"][:, 0:32], t["identf"][:, 32:64], ALU.add))
                link(dve.tensor_tensor(t["sel"][:, :], t["sel"][:, :], t["identf"][:, 64:96], ALU.add))
                link(dve.tensor_tensor(t["sel"][:, :], t["sel"][:, :], t["identf"][:, 96:128], ALU.add))
                dve.wait_ge(s_wr, 16 * 3 * P // C)
                scale = float(D) ** -0.25
                for w in range(3):
                    ins = dve.scalar_tensor_tensor(
                        out=wbd[:, w, :].rearrange("p (h o) -> p h o", o=C), in0=onb[:, :, :],
                        scalar=scale if w < 2 else 1.0, in1=wrep[:, w, :].unsqueeze(1).broadcast_to([P, P // C, C]),
                        op0=ALU.mult, op1=ALU.mult)
                ins.then_inc(s_wbd, 1)

                def modulation():
                    dve.wait_ge(s_modp, 1)
                    link(dve.tensor_copy(t["mod"][:, :], modp[:, 0:12]))
                    for j in (1, 4):
                        dve.tensor_scalar(t["mod"][:, 2 * j:2 * j + 2], t["mod"][:, 2 * j:2 * j + 2],
                                          1.0, None, ALU.add).then_inc(s_mod, 1)

                def gates():
                    floor_gate(t["mod"][:, 10:12], gbt)
                    link(dve.tensor_copy(t["gb"][:, :], gbt[:, 0, :]))
                    link(dve.tensor_copy(gtmp[:, 0, :], modp[0:1, 16:16 + D]))
                    floor_gate(gtmp[:, 0, :], gtmp)
                    link(dve.tensor_copy(grow[:, 0:D], gtmp[:, 0, :]))
                    dve.wait_ge(s_bu, 16)
                    dve.tensor_tensor(grow[:, D:2 * D], gtmp[:, 0, :], burow[:, :], ALU.mult).then_inc(s_mod, 1)

                def floor_gate(src, b):
                    link(dve.tensor_scalar(b[:, 1, :], src, -1.0, None, ALU.mult))
                    link(dve.tensor_tensor(b[:, 1, :], b[:, 1, :], src, ALU.max))
                    link(dve.tensor_scalar(b[:, 2, :], src, 0.0, 2.0, ALU.is_ge, ALU.mult))
                    link(dve.tensor_scalar(b[:, 2, :], b[:, 2, :], -1.0, None, ALU.add))
                    link(dve.tensor_scalar(b[:, 1, :], b[:, 1, :], FLOOR, None, ALU.max))
                    link(dve.tensor_tensor(b[:, 0, :], b[:, 1, :], b[:, 2, :], ALU.mult))

                def statistics(g):
                    dve.wait_ge(s_x[g], 16)
                    ts = range(g * GT, (g + 1) * GT)
                    for i in ts:
                        ins = dve.bn_stats(stats[:, i, :], t["x"][:, i, :])
                    link(ins)
                    for i in ts:
                        ins = dve.bn_aggr(mv[:, i, :], stats[:, i, :])
                    link(ins)
                    dve.tensor_scalar(ve[:, ts[0]:ts[-1] + 1], mv[:, ts[0]:ts[-1] + 1, 1], EPS, None,
                                      ALU.add).then_inc(s_ve, 1)

                def normalised(b):
                    dve.wait_ge(s_rstd, b // 2 + 1)
                    if b >= 2:
                        dve.wait_ge(s_tp, NS * (b - 1))
                    for i in range(TPB * b, TPB * (b + 1)):
                        dve.tensor_scalar(xn[:, b % 2, i % TPB, :], t["x"][:, i, :], mv[:, i, 0:1], rstd[:, i:i + 1],
                                          ALU.subtract, ALU.mult).then_inc(s_xn, 1)

                def rests(b):
                    for c in range(4 * b, 4 * b + 4):
                        i = c % QKR
                        dve.wait_ge(s_p1, c + 1)
                        if c >= QKR:
                            dve.wait_ge(s_p3, c - QKR + 1)
                        dve.tensor_tensor(rest[:, i, :], qk[i][:, :], parts[:, i, 0, :], ALU.subtract).then_inc(s_r, 1)

                statistics(0)
                modulation()
                normalised(0)
                statistics(1)
                normalised(1)
                gates()
                for b in range(NB):
                    if b % 2 == 0 and b // 2 + 2 < 4:
                        statistics(b // 2 + 2)
                    if b + 2 < NB:
                        normalised(b + 2)
                    rests(b)
                dve.wait_ge(s_bc, 1)
                dve.tensor_copy(t["gab"][:, :], modp[:, :])

            @block.scalar
            def _(act):
                for w, name in enumerate(("WqT", "WkT", "WvT")):
                    for h in range(P // C):
                        act.dma_start(wrep[h * C:(h + 1) * C, w, :], d[name]).then_inc(s_wr, 16)
                act.dma_start(burow[:, :], d["bu"].rearrange("(a n) -> a n", a=1)).then_inc(s_bu, 16)
                act.wait_ge(s_c, 16)
                act.activation(scol[:, :], ccol[:, :], ACT.Silu).then_inc(s_silu, 1)
                act.wait_ge(s_mod, 2)

                def modulated(b):
                    for s in range(NS):
                        act.wait_ge(s_tp, NS * b + s + 1)
                        act.activation(hT[:, b, s, :], tp[s][:, :], ACT.Identity,
                                       scale=t["mod"][:, 2 + s:3 + s], bias=t["mod"][:, s:s + 1]).then_inc(s_hT, 1)

                def part2(c):
                    i = c % QKR
                    act.wait_ge(s_r, c + 1)
                    act.activation(parts[:, i, 1, :], rest[:, i, :], ACT.Copy).then_inc(s_p2, 1)

                modulated(0)
                for c, (b, s, w) in enumerate(chunks):
                    i = c % QKR
                    if c % 4 == 0 and b + 1 < NB:
                        modulated(b + 1)
                    act.wait_ge(s_qk, c + 1)
                    if c >= QKR:
                        act.wait_ge(s_store[i], 16 * (c // QKR))
                    act.activation(parts[:, i, 0, :], qk[i][:, :], ACT.Copy).then_inc(s_p1, 1)
                    if c >= 1:
                        part2(c - 1)
                part2(len(chunks) - 1)

            @block.tensor
            def _(pe):
                pe.wait_ge(s_silu, 1)
                pe.wait_ge(s_wm, 16)
                for j in range(12):
                    for s in range(NS):
                        pe.matmul(modp[:, j:j + 1], wmod[:, s, j * P:(j + 1) * P], scol[:, s:s + 1],
                                  start=(s == 0), stop=(s == NS - 1))
                for s in range(NS):
                    ins = pe.matmul(modp[0:1, 16:16 + D], scol[:, s:s + 1], wmod[:, s, 2 * D:3 * D],
                                    start=(s == 0), stop=(s == NS - 1))
                ins.then_inc(s_modp, 1)
                pe.wait_ge(s_const, 2)
                pe.wait_ge(s_wbd, 1)

                def turn(b):
                    pe.wait_ge(s_xn, TPB * (b + 1))
                    for s in range(NS):
                        if b:
                            pe.wait_ge(s_hT, NS * (b - 1) + s + 1)
                        for i in range(TPB):
                            ins = pe.transpose(tp[s][:, i * P:(i + 1) * P],
                                               xn[:, b % 2, i, s * P:(s + 1) * P], t["identf"][:, :])
                        ins.then_inc(s_tp, 1)

                turn(0)
                for c, (b, s, w) in enumerate(chunks):
                    if c % 4 == 0:
                        if b + 1 < NB:
                            turn(b + 1)
                        pe.wait_ge(s_hT, 2 * b + 2)
                    if c >= QKR:
                        pe.wait_ge(s_r, c - QKR + 1)
                    pe.matmul(qk[c % QKR][:, :], wbd[:, w, :], hT[:, b, s, :],
                              start=True, stop=True).then_inc(s_qk, 1)
                pe.wait_ge(s_mod, 3)
                pe.matmul(modp[:, :], ones1[:, :], grow[:, :], start=True, stop=True).then_inc(s_bc, 1)


PV_LAG, YO_LAG, MT_LAG = 6, 5, 9
UNITS = [(slot, j, k) for slot in (0, 1) for j in range(NB) for k in range(TPB * (j + 1))]
NU = len(UNITS)
WRAP = 12


def tile_jobs(slot, j):
    jobs = []
    for r in range(TPB):
        keys = (TPB * j + r + 1) * P
        for c in range(-(-keys // (SW * BW))):
            jobs.append((slot, j, r, c, c * SW * BW, min(keys, (c + 1) * SW * BW)))
    return [(x, i == len(jobs) - 1) for i, x in enumerate(jobs)]


def schedule():
    ahead = [job for j in range(LEAD) for job in tile_jobs(0, j)]
    pair = [job for slot, j in [(0, j) for j in range(LEAD, NB)] + [(1, j) for j in range(NB)] +
            [(0, j) for j in range(LEAD)] for job in tile_jobs(slot, j)]
    cost = [x[5] - x[4] + 200 for x, _ in pair]
    events, later, sent = [], [], 0

    def maxima(job, at):
        nonlocal later, sent
        x, last = job
        if last:
            due = [e for _, e in later if e[0] == "MT"][:-(M_SLOTS - 2)]
            events.extend(due)
            later = [(w, e) for w, e in later if e not in due]
        events.append(("S", (sent, x, last)))
        sent += 1
        if last:
            later.append((at + MT_LAG, ("MT", (x[0], x[1]))))

    for i, job in enumerate(ahead):
        maxima(job, -MT_LAG)
        if i % 3 == 2 and i // 3 < NT // 2:
            events.append(("VP", i // 3))
    assert len(ahead) // 3 >= NT // 2
    events.append(("V", 0))
    events += [e for _, e in later]
    later = []
    cut, spent, n = 0, 0, 0
    for s in range(NU + WRAP):
        if s == WRAP:
            cut = len(events)
        if s == NU:
            assert n == len(pair)
            spent, n = 0, 0
        events += [e for at, e in later if at == s]
        later = [(at, e) for at, e in later if at != s]
        slot, j, k = UNITS[s % NU]
        early = [e for _, e in later if k == 0 and e == ("MT", (slot, j))]
        events += early
        later = [(at, e) for at, e in later if e not in early]
        events.append(("ST", (s, slot, j, k)))
        if k == TPB * NB - 1:
            later.append((s + 3, ("FREE", slot)))
        if k == 3 and j == 3:
            later.append((s + 1, ("V", 1 - slot)))
        if s >= WRAP and (s - WRAP) % (NU // 4) == 0:
            events.append(("X", (s - WRAP) // (NU // 4)))
        g = s - PV_LAG
        if g >= 0 and g % TPB == 0:
            slot, j, k = UNITS[g % NU]
            events.append(("PV", (g // TPB, slot, j, k // TPB)))
            if k // TPB == j:
                later += [(s + 1, ("OD", (slot, j))), (s + 1 + YO_LAG, ("YO", (slot, j)))]
        while n < len(pair) and spent <= sum(cost) * (s % NU + 1) / NU:
            maxima(pair[n], s)
            spent += cost[n]
            n += 1
    assert not [e for e in events[:cut] if e[0] in ("YO", "FREE")]
    return events[:cut], events[cut:]


class Ledger:

    def __init__(self, eng, sems):
        self.eng, self.sems = eng, sems
        self.n, self.seen, self.base = {}, {}, {}

    def raised(self, name, by=1):
        self.n[name] = self.n.get(name, 0) + by
        return self.n[name]

    def wait(self, name, mark=None):
        mark = self.n.get(name, 0) if mark is None else mark
        if mark > self.seen.get(name, 0):
            self.seen[name] = mark
            self.eng.wait_ge(self.sems[name], mark - self.base.get(name, 0))

    def settle(self):
        self.eng.drain()
        for name in sorted(self.seen):
            by = self.seen[name] - self.base.get(name, 0)
            if by:
                self.eng.nop().then_inc(self.sems[name], -by)
            self.base[name] = self.seen[name]

    def ahead(self):
        return {name: n - self.base.get(name, 0) for name, n in self.n.items()}


def attend(nc, t, d):
    with ExitStack() as ctx:
        def sb(name, shape, dt):
            return ctx.enter_context(nc.sbuf_tensor(name, shape, dt))

        NP = 8
        prob = sb("prob", [P, NP, BW], F32)
        mx = sb("mx", [P, M_SLOTS, TPB, NB // SW], F32)
        mq = sb("mq", [P, M_SLOTS, TPB], F32)
        nm = sb("nm", [P, M_SLOTS, TPB], F32)
        mt = sb("mt", [P, M_SLOTS, TPB, 2], BF16)
        od = sb("od", [P, 2, BW], F32)
        rl = sb("rl", [P, 2, TPB], F32)
        tok = sb("tok", [1, 2], F32)
        S = [ctx.enter_context(nc.psum_tensor(f"S{i}", [P, SW * BW], F32)) for i in range(S_SLOTS)]
        ST = [ctx.enter_context(nc.psum_tensor(f"ST{i}", [P, BW], F32)) for i in range(ST_SLOTS)]
        O = ctx.enter_context(nc.psum_tensor("O", [P, BW], F32))
        M = ctx.enter_context(nc.psum_tensor("M", [P, BW], F32))
        names = ("s_full", "s_read", "s_last_read", "st_full", "exp_done", "pv_done", "od_done", "m_full",
                 "m_split", "mt_full", "m_copied", "y_full", "y_done", "v_full", "dve_chain", "pool_chain",
                 "heads_free", "stack0", "stack1", "y_chain")
        q = {n: ctx.enter_context(nc.semaphore("at_" + n)) for n in names}
        s_vp, s_vc = ctx.enter_context(nc.semaphore("vp_full")), ctx.enter_context(nc.semaphore("v_copied"))
        qst, kst, vpad = t["qst"], t["kst"], t["vpad"]

        prologue, turn = schedule()

        def run(eng, section, over=()):
            def part(events, h):
                section(events, led, h)
                for name in over:
                    led.wait(name)
                led.settle()

            led = Ledger(eng, q)
            part(prologue, 0)
            before = led.ahead()
            with eng.Fori(0, H // 2) as pair:
                part(turn, pair * 2)
            after = led.ahead()
            assert all(after[k] == before.get(k, 0) for k in after), (before, after)

        LOADED = 16 * (len(QPARTS) + len(KPARTS))

        def load(sp, slot, head):
            row = head * C
            for name, st, parts in (("qs", qst[slot], QPARTS), ("ks", kst[slot], KPARTS)):
                for i, k in enumerate(parts):
                    sp.dma_start(st[i * C:(i + 1) * C, :], d[name][k, bass.ds(row, C), :]
                                 ).then_inc(q[f"stack{slot}"], 16)

        with nc.Block() as block:
            @block.sync
            def _(sp):
                load(sp, 0, 0)
                sp.sem_inc(q["heads_free"], 1)
                with sp.Fori(0, H // 2) as pair:
                    h = pair * 2
                    for n, slot in enumerate((1, 0)):
                        sp.wait_ge(q["heads_free"], n + 1)
                        load(sp, slot, h + 1 + n)
                    sp.drain()
                    sp.nop().then_inc(q["heads_free"], -2)

            @block.tensor
            def _(pe):
                read = []
                mrow = {}

                def section(events, led, _):
                    if not read:
                        led.raised("stack0", LOADED)
                        led.wait("stack0")
                    for kind, e in events:
                        if kind == "S":
                            n, (slot, j, r, c, k0, k1), last = e
                            if read and j == 0 and r == 0:
                                led.raised(f"stack{slot}", LOADED)
                                led.wait(f"stack{slot}")
                            if n >= S_SLOTS:
                                led.wait(*read[n - S_SLOTS])
                            src = "s_last_read" if last else "s_read"
                            read.append((src, led.raised(src)))
                            qc = (TPB * j + r) * P
                            for a in range(k0, k1, BW):
                                b = min(a + BW, k1)
                                diag = b == qc + P
                                ins = pe.matmul(S[n % S_SLOTS][:, a - k0:b - k0], qst[slot][0:ROWS, qc:qc + P],
                                                kst[slot][0:ROWS, a:b], start=True, stop=not diag)
                                if diag:
                                    ins = pe.matmul(S[n % S_SLOTS][:, b - P - k0:b - k0], t["identb"][:, :],
                                                    t["maskq"][:, :], start=False, stop=True)
                            ins.then_inc(q["s_full"], 1)
                        elif kind == "VP":
                            if e >= ST_SLOTS:
                                pe.wait_ge(s_vc, e - ST_SLOTS + 1)
                            for i in range(2):
                                n = 2 * e + i
                                for s in range(NS):
                                    ins = pe.matmul(ST[e % ST_SLOTS][:, i * D + s * P:i * D + (s + 1) * P],
                                                    t["h2"][:, n // TPB, s, n % TPB * P:(n % TPB + 1) * P],
                                                    t["wbd"][:, 2, :], start=True, stop=True)
                            ins.then_inc(s_vp, 1)
                        elif kind == "MT":
                            slot, j = e
                            led.raised("mt_full")
                            led.wait("mt_full")
                            led.wait("m_copied")
                            led.wait("y_done")
                            for i in range(TPB):
                                ins = pe.matmul(M[ROWS:SROWS, i * P:(i + 1) * P], mt[:, j % M_SLOTS, i, :],
                                                t["identb"][:, :], start=True, stop=True)
                            ins.then_inc(q["m_split"], 1)
                            mrow[e] = led.raised("m_copied")
                        elif kind == "ST":
                            s, slot, j, k = e
                            if k == 0:
                                led.wait("m_copied", mrow[(slot, j)])
                            if s == 0:
                                pe.wait_ge(s_vc, NT // 2)
                            led.wait("exp_done", s - ST_SLOTS + 1)
                            c0 = max(0, k - TPB * j) * P
                            diag = k >= TPB * j
                            q0 = j * BW
                            ins = pe.matmul(ST[s % ST_SLOTS][:, c0:BW], kst[slot][0:SROWS, k * P:(k + 1) * P],
                                            qst[slot][0:SROWS, q0 + c0:q0 + BW], start=True, stop=not diag)
                            if diag:
                                ins = pe.matmul(ST[s % ST_SLOTS][:, c0:c0 + P], t["identb"][:, :],
                                                t["maskk"][:, :], start=False, stop=True)
                            ins.then_inc(q["st_full"], 1)
                            led.raised("exp_done")
                        elif kind == "PV":
                            g, slot, j, G = e
                            if G == 0:
                                led.wait("od_done")
                                if j == 0:
                                    led.raised("v_full")
                                    led.wait("v_full")
                            led.wait("exp_done", TPB * (g + 1))
                            for r in range(TPB):
                                k = TPB * G + r
                                c0 = r * P if G == j else 0
                                row = 32 * r if j else 0
                                ins = pe.matmul(O[row:row + 32, c0:BW], vpad[slot][:, k, :],
                                                prob[:, (TPB * g + r) % NP, c0:BW],
                                                start=(G == 0 if j else r == 0),
                                                stop=(G == j if j else r == 3), tile_position=(0, row),
                                                skip_group_check=True)
                            ins.then_inc(q["pv_done"], 1)
                            if G == j:
                                led.raised("od_done")
                        elif kind == "YO":
                            slot, j = e
                            led.wait("od_done")
                            led.wait("m_copied")
                            led.wait("y_done")
                            rows = P if j else 32
                            for i in range(TPB):
                                ins = pe.matmul(M[:, 32 * i:32 * i + 32], od[0:rows, j % 2, i * P:(i + 1) * P],
                                                t["sel"][0:rows, :], start=True, stop=True)
                            ins.then_inc(q["y_full"], 1)
                            led.raised("y_done")

                run(pe, section, over=("m_copied", "y_done"))

            @block.scalar
            def _(act):
                def vcopy(slot, head):
                    act.activation(vpad[slot][:, :, 0:C], t["v"][:, :, bass.ds(head * C, C)],
                                   ACT.Copy).then_inc(q["v_full"], 1)

                def section(events, led, h):
                    for kind, e in events:
                        if kind == "VP":
                            act.wait_ge(s_vp, e + 1)
                            act.activation(t["v"][:, 2 * e:2 * e + 2, 0:D],
                                           ST[e % ST_SLOTS][:, :].rearrange("p (a n) -> p a n", a=2),
                                           ACT.Copy).then_inc(s_vc, 1)
                        elif kind == "MT":
                            slot, j = e
                            led.raised("m_split")
                            led.wait("m_split")
                            act.activation(qst[slot][ROWS:SROWS, j * BW:(j + 1) * BW], M[ROWS:SROWS, :],
                                           ACT.Copy).then_inc(q["m_copied"], 1)
                        elif kind == "ST":
                            s, slot, j, k = e
                            led.raised("st_full")
                            led.wait("st_full")
                            if s % TPB == 0:
                                led.wait("pv_done", (s - NP) // TPB + 1)
                            c0 = max(0, k - TPB * j) * P
                            act.activation(prob[:, s % NP, c0:BW], ST[s % ST_SLOTS][:, c0:BW],
                                           ACT.Exp).then_inc(q["exp_done"], 1)
                        elif kind == "PV":
                            led.raised("pv_done")
                        elif kind == "OD":
                            slot, j = e
                            led.wait("pv_done")
                            rows = P if j else 32
                            act.activation(od[0:rows, j % 2, :], O[0:rows, :], ACT.Copy).then_inc(q["od_done"], 1)
                        elif kind == "V":
                            if events is prologue:
                                act.wait_ge(s_vc, NT // 2)
                                vcopy(0, 0)
                            else:
                                vcopy(e, h + (1 if e else 2))
                        elif kind == "FREE":
                            act.activation(tok[:, 0:1], t["mod"][0:1, 0:1], ACT.Copy).then_inc(q["heads_free"], 1)

                run(act, section)

            @block.vector
            def _(dve):
                def section(events, led, h):
                    for kind, e in events:
                        if kind == "S":
                            n, (slot, j, r, c, k0, k1), last = e
                            led.raised("s_full")
                            led.wait("s_full")
                            ins = dve.tensor_reduce(mx[:, j % M_SLOTS, r, c:c + 1], S[n % S_SLOTS][:, 0:k1 - k0],
                                                    AX_X, ALU.max)
                            if not last:
                                ins.then_inc(q["s_read"], 1)
                                continue
                            ins.then_inc(q["dve_chain"], 1)
                            led.raised("dve_chain")
                            led.wait("dve_chain")
                            dve.tensor_reduce(mq[:, j % M_SLOTS, :], mx[:, j % M_SLOTS, :, 0:c + 1], AX_X,
                                              ALU.max).then_inc(q["m_full"], 1)
                        elif kind == "YO":
                            slot, j = e
                            led.raised("y_full")
                            led.wait("y_full")
                            y = M[:, 0:32 * TPB].rearrange("p (a c) -> p a c", c=32)
                            dve.reciprocal(rl[:, j % 2, :], y[:, :, C]).then_inc(q["y_chain"], 1)
                            led.raised("y_chain")
                            led.wait("y_chain")
                            dve.tensor_tensor(
                                t["y"][:, TPB * j:TPB * j + TPB, bass.ds((h + slot) * C, C)], y[:, :, 0:C],
                                rl[:, j % 2, :].unsqueeze(2).broadcast_to([P, TPB, C]),
                                ALU.mult).then_inc(q["y_done"], 1)

                run(dve, section)

            @block.gpsimd
            def _(pool):
                def section(events, led, h):
                    for kind, e in events:
                        if kind == "X":
                            x = t["x"][:, bass.ds(h * 2 + e, 1), :].rearrange("p a n -> p (a n)")
                            pool.tensor_tensor(x, x, t["gab"][:, D:2 * D], ALU.add)
                        elif kind == "S" and e[2]:
                            j = e[1][1] % M_SLOTS
                            led.raised("m_full")
                            led.wait("m_full")
                            pool.tensor_scalar(nm[:, j, :], mq[:, j, :], -1.0, None,
                                               ALU.mult).then_inc(q["s_last_read"], 1)
                            pool.tensor_scalar(mt[:, j, :, 0], mq[:, j, :], -1.0, None,
                                               ALU.mult).then_inc(q["pool_chain"], 1)
                            led.raised("pool_chain")
                            led.wait("pool_chain")
                            pool.tensor_tensor(mt[:, j, :, 1], nm[:, j, :], mt[:, j, :, 0],
                                               ALU.subtract).then_inc(q["mt_full"], 1)

                run(pool, section)


def project(nc, t, d):
    with ExitStack() as ctx:
        def sb(name, shape, dt):
            return ctx.enter_context(nc.sbuf_tensor(name, shape, dt))

        def sem(name):
            return ctx.enter_context(nc.semaphore(name))

        WR = 3
        QT = 2 * TPB
        cuts = [[u for u in range(U) if u * NB // U == b] for b in range(NB)]
        wraw = sb("wraw", [P, WR, WU], F32)
        wu = sb("wu", [P, NS, D], F32)
        gwT = sb("gwT", [P, NS, E], F32)
        bias = sb("bias", [P, E], F32)
        yT = sb("yT", [P, NS, BW], F32)
        xn = sb("xn2", [P, 2, TPB, D], F32)
        stats = sb("stats2", [P, 2, TPB, 6], F32)
        mv = sb("mv2", [P, 2, TPB, 2], F32)
        ve = sb("ve2", [P, 2, TPB], F32)
        rstd = sb("rstd2", [P, 2, TPB], F32)
        half = sb("half2", [P, TPB], F32)
        sc = sb("sc", [P, NT, E], F32)
        sfc = sb("sfc", [P, QT, E], F32)
        left = sb("left", [P, QT, E], F32)
        gs = sb("gs", [P, QT, NG], F32)
        grank = sb("grank", [P, QT, NG], F32)
        gtmp = sb("gtmp2", [P, QT, NG], F32)
        top = sb("top", [P, QT, 8], F32)
        wsum = sb("wsum", [P, QT], F32)
        cwe = sb("cwe", [P, 4, P], F32)
        cwT = sb("cwT", [P, 4, P], F32)
        tpy = [ctx.enter_context(nc.psum_tensor(f"tpy{i}", [P, BW], F32)) for i in range(2)]
        pj = [ctx.enter_context(nc.psum_tensor(f"pj{i}", [P, BW], F32)) for i in range(2)]
        tpx = [ctx.enter_context(nc.psum_tensor(f"tpx{i}", [P, BW], F32)) for i in range(2)]
        gl = [ctx.enter_context(nc.psum_tensor(f"gl{i}", [P, 2, P], F32)) for i in range(2)]

        s_w = [sem(f"wraw_in{i}") for i in range(WR)]
        s_wu, s_gw, s_bias, s_x1, s_cwo = sem("wu_in"), sem("gw_in"), sem("bias_in"), sem("x1_out"), sem("cw_out")
        s_hi, s_dve, s_cut, s_half = sem("high_parts"), sem("dve_chain2"), sem("cut"), sem("half_ready")
        s_tpy, s_yT, s_wus, s_pj, s_x1r = sem("tpy"), sem("yT_ready"), sem("wu_scaled"), sem("pj"), sem("x1_ready")
        s_ve, s_rstd, s_xn, s_tpx, s_h2 = sem("ve_ready"), sem("rstd_ready"), sem("xn_ready"), sem("tpx"), sem("h2_ready")
        s_gl, s_sig, s_cw, s_tpc, s_cwT = sem("gl"), sem("sigmoid"), sem("cw_ready"), sem("tpc"), sem("cwT_ready")
        whi, wlo = t["whi"], t["wlo"]

        STEPS = NB + 5

        with nc.Block() as block:
            @block.sync
            def _(sp):
                for u in range(U):
                    if u >= WR:
                        sp.wait_ge(s_cut, u - WR + 1)
                    sp.dma_start(wraw[:, u % WR, :], d["wcat"][u]).then_inc(s_w[u % WR], 16)

            @block.scalar
            def _(act):
                act.dma_start(wu[:, :, :], d["WuT"].rearrange("(s p) n -> p s n", p=P)).then_inc(s_wu, 16)
                act.dma_start(gwT[:, :, :], d["gwT"].rearrange("(s p) n -> p s n", p=P)).then_inc(s_gw, 16)
                act.dma_start(bias[:, :], d["gbias"].unsqueeze(0).broadcast_to([P, E])).then_inc(s_bias, 16)

                def turned(b):
                    if b >= 1:
                        act.wait_ge(s_pj, 2 * b)
                    for s in range(NS):
                        act.wait_ge(s_tpy, NS * b + s + 1)
                        act.activation(yT[:, s, :], tpy[s][:, :], ACT.Copy).then_inc(s_yT, 1)

                def sigmoid(g):
                    act.wait_ge(s_gl, g + 1)
                    act.activation(sc[:, g * QT:(g + 1) * QT, :],
                                   gl[g % 2][:, 0, :].rearrange("p (a n) -> p a n", n=E),
                                   ACT.Sigmoid).then_inc(s_sig, 1)

                def weights(g):
                    act.wait_ge(s_tpc, g + 1)
                    act.activation(cwT[:, g, :], gl[g % 2][:, 1, :], ACT.Copy).then_inc(s_cwT, 1)
                    act.wait_ge(s_cwT, g + 1)
                    dst = d["cw"][g].rearrange("e (a k) -> (e a) k", k=P)
                    act.dma_start(dst, cwT[:, g, :]).then_inc(s_cwo, 16)

                def high(u):
                    act.wait_ge(s_w[u % WR], 16 * (u // WR + 1))
                    act.activation(whi[:, u, :], wraw[:, u % WR, :], ACT.Copy).then_inc(s_hi, 1)

                def modulated(b):
                    for s in range(NS):
                        act.wait_ge(s_tpx, NS * b + s + 1)
                        act.activation(t["h2"][:, b, s, :], tpx[s][:, :], ACT.Identity,
                                       scale=t["mod"][:, 8 + s:9 + s],
                                       bias=t["mod"][:, 6 + s:7 + s]).then_inc(s_h2, 1)
                    act.wait_ge(s_x1r, 2 * (b + 1))
                    act.dma_start(d["x1"][b], t["x"][:, TPB * b:TPB * b + TPB, :].rearrange(
                        "p a n -> p (a n)")).then_inc(s_x1, 16)

                for k in range(STEPS):
                    if k < NB:
                        turned(k)
                    if 0 < k <= NB:
                        for u in cuts[k - 1]:
                            high(u)
                    if 0 <= k - 3 < NB:
                        modulated(k - 3)
                    if k >= 5 and k % 2:
                        sigmoid((k - 5) // 2)
                    if k >= 6 and k % 2 == 0:
                        weights((k - 6) // 2)
                act.wait_ge(s_x1, 16 * NB)
                act.wait_ge(s_cwo, 64)

            @block.gpsimd
            def _(pool):
                pool.memset(half[:, :], -0.5).then_inc(s_half, 1)
                pool.wait_ge(s_half, 1)
                for b in range(NB):
                    pool.wait_ge(s_ve, b + 1)
                    pool.tensor_tensor(rstd[:, b % 2, :], ve[:, b % 2, :], half[:, :], ALU.pow).then_inc(s_rstd, 1)
                    for u in cuts[b]:
                        pool.wait_ge(s_hi, u + 1)
                        pool.tensor_tensor(wlo[:, u, :], wraw[:, u % WR, :], whi[:, u, :],
                                           ALU.subtract).then_inc(s_cut, 1)

            @block.vector
            def _(dve):
                n = [0]

                def link(ins):
                    n[0] += 1
                    ins.then_inc(s_dve, 1)
                    dve.wait_ge(s_dve, n[0])

                dve.wait_ge(s_wu, 16)
                for s in range(NS):
                    dve.tensor_tensor(wu[:, s, :], wu[:, s, :], t["gab"][:, 0:D], ALU.mult).then_inc(s_wus, 1)

                def residual(b):
                    for i in range(2):
                        dve.wait_ge(s_pj, 2 * b + i + 1)
                        x = t["x"][:, TPB * b + 2 * i:TPB * b + 2 * i + 2, :]
                        dve.tensor_tensor(x, x, pj[i][:, :].rearrange("p (a n) -> p a n", a=2),
                                          ALU.add).then_inc(s_x1r, 1)
                    dve.wait_ge(s_x1r, 2 * b + 2)
                    for i in range(TPB):
                        ins = dve.bn_stats(stats[:, b % 2, i, :], t["x"][:, TPB * b + i, :])
                    link(ins)
                    for i in range(TPB):
                        ins = dve.bn_aggr(mv[:, b % 2, i, :], stats[:, b % 2, i, :])
                    link(ins)
                    dve.tensor_scalar(ve[:, b % 2, :], mv[:, b % 2, :, 1], EPS, None, ALU.add).then_inc(s_ve, 1)

                def normalised(b):
                    dve.wait_ge(s_rstd, b + 1)
                    if b >= 2:
                        dve.wait_ge(s_tpx, NS * (b - 1))
                    for i in range(TPB):
                        dve.tensor_scalar(xn[:, b % 2, i, :], t["x"][:, TPB * b + i, :], mv[:, b % 2, i, 0:1],
                                          rstd[:, b % 2, i:i + 1], ALU.subtract, ALU.mult).then_inc(s_xn, 1)

                def router(g):
                    score = sc[:, g * QT:(g + 1) * QT, :]
                    dve.wait_ge(s_sig, g + 1)
                    dve.wait_ge(s_bias, 16)
                    link(dve.tensor_tensor(sfc[:, :, :], score, bias[:, :].unsqueeze(1).broadcast_to([P, QT, E]),
                                           ALU.add))
                    g4 = sfc[:, :, :].rearrange("p t (g k) -> p t g k", k=E // NG)
                    pairs = [(a, b) for a in range(4) for b in range(a + 1, 4)]
                    for m, (a, b) in enumerate(pairs):
                        dst = gtmp if m else gs
                        link(dve.tensor_tensor(dst[:, :, :], g4[:, :, :, a], g4[:, :, :, b], ALU.add))
                        if m:
                            link(dve.tensor_tensor(gs[:, :, :], gs[:, :, :], gtmp[:, :, :], ALU.max))
                    for i in range(NG):
                        ins = dve.memset(grank[:, :, i:i + 1], float(NG - 1 - i))
                    link(ins)
                    for k in range(1, NG):
                        n = NG - k
                        link(dve.tensor_tensor(gtmp[:, :, 0:n], gs[:, :, 0:n], gs[:, :, k:NG], ALU.is_ge))
                        link(dve.tensor_tensor(grank[:, :, k:NG], grank[:, :, k:NG], gtmp[:, :, 0:n], ALU.add))
                        link(dve.tensor_tensor(grank[:, :, 0:n], grank[:, :, 0:n], gtmp[:, :, 0:n], ALU.subtract))
                    link(dve.tensor_scalar(gtmp[:, :, :], grank[:, :, :], float(TG) - 0.5, None, ALU.is_lt))
                    keep = gtmp[:, :, :].unsqueeze(3).broadcast_to([P, QT, NG, E // NG])
                    link(dve.tensor_tensor(g4, g4, keep, ALU.mult))
                    link(dve.tensor_scalar(gtmp[:, :, :], gtmp[:, :, :], -1.0, -MASKED, ALU.add, ALU.mult))
                    link(dve.tensor_tensor(g4, g4, keep, ALU.add))
                    for i in range(QT):
                        ins = dve.max(top[:, i, :], sfc[:, i, :])
                    link(ins)
                    link(dve.memset(top[:, :, TOPK:8], MASKED))
                    for i in range(QT):
                        ins = dve.match_replace(left[:, i, :], top[:, i, :], sfc[:, i, :], MASKED)
                    link(ins)
                    link(dve.tensor_tensor(left[:, :, :], sfc[:, :, :], left[:, :, :], ALU.is_gt))
                    link(dve.tensor_tensor(score, score, left[:, :, :], ALU.mult))
                    link(dve.tensor_reduce(wsum[:, :], score, AX_X, ALU.add))
                    link(dve.tensor_scalar(wsum[:, :], wsum[:, :], 1e-20, None, ALU.add))
                    link(dve.reciprocal(wsum[:, :], wsum[:, :]))
                    link(dve.tensor_scalar(wsum[:, :], wsum[:, :], RSCALE, None, ALU.mult))
                    dve.tensor_tensor(cwe[:, g, :].rearrange("p (e a) -> p a e", e=E), score,
                                      wsum[:, :].unsqueeze(2).broadcast_to([P, QT, E]), ALU.mult).then_inc(s_cw, 1)

                for k in range(STEPS):
                    if 0 <= k - 1 < NB:
                        residual(k - 1)
                    if 0 <= k - 2 < NB:
                        normalised(k - 2)
                    if k >= 5 and k % 2:
                        router((k - 5) // 2)

            @block.tensor
            def _(pe):
                def turn(b):
                    for s in range(NS):
                        if b >= 1:
                            pe.wait_ge(s_yT, NS * (b - 1) + s + 1)
                        for i in range(TPB):
                            ins = pe.transpose(tpy[s][:, i * P:(i + 1) * P],
                                               t["y"][:, TPB * b + i, s * P:(s + 1) * P], t["identf"][:, :])
                        ins.then_inc(s_tpy, 1)

                def proj(b):
                    pe.wait_ge(s_yT, NS * (b + 1))
                    for i in range(TPB):
                        if b >= 1 and i % 2 == 0:
                            pe.wait_ge(s_x1r, 2 * (b - 1) + i // 2 + 1)
                        for s in range(NS):
                            ins = pe.matmul(pj[i // 2][:, (i % 2) * D:(i % 2 + 1) * D],
                                            yT[:, s, i * P:(i + 1) * P], wu[:, s, :],
                                            start=(s == 0), stop=(s == NS - 1))
                        if i % 2:
                            ins.then_inc(s_pj, 1)

                def normed(b):
                    pe.wait_ge(s_xn, TPB * (b + 1))
                    for s in range(NS):
                        if b >= 1:
                            pe.wait_ge(s_h2, NS * (b - 1) + s + 1)
                        for i in range(TPB):
                            ins = pe.transpose(tpx[s][:, i * P:(i + 1) * P], xn[:, b % 2, i, s * P:(s + 1) * P],
                                               t["identf"][:, :])
                        ins.then_inc(s_tpx, 1)

                def logits(b):
                    pe.wait_ge(s_h2, NS * (b + 1))
                    if b >= 4:
                        pe.wait_ge(s_cwT, b // 2 - 1)
                    for i in range(TPB):
                        n = b % 2 * TPB + i
                        for s in range(NS):
                            ins = pe.matmul(gl[b // 2 % 2][:, 0, n * E:(n + 1) * E],
                                            t["h2"][:, b, s, i * P:(i + 1) * P], gwT[:, s, :],
                                            start=(s == 0), stop=(s == NS - 1))
                    if b % 2:
                        ins.then_inc(s_gl, 1)

                def weights(g):
                    pe.wait_ge(s_cw, g + 1)
                    pe.transpose(gl[g % 2][:, 1, :], cwe[:, g, :], t["identf"][:, :]).then_inc(s_tpc, 1)

                for k in range(STEPS):
                    if k < NB:
                        turn(k)
                    if k == 1:
                        pe.wait_ge(s_wus, NS)
                        pe.wait_ge(s_gw, 16)
                    if 0 <= k - 1 < NB:
                        proj(k - 1)
                    if 0 <= k - 3 < NB:
                        normed(k - 3)
                    if 0 <= k - 4 < NB:
                        logits(k - 4)
                    if k >= 6 and k % 2 == 0:
                        weights((k - 6) // 2)


def experts(nc, t, d):
    with ExitStack() as ctx:
        def sb(name, shape, dt):
            return ctx.enter_context(nc.sbuf_tensor(name, shape, dt))

        whi, wlo, h2 = t["whi"], t["wlo"], t["h2"]
        HC = E // 4
        hhi = sb("hhi", [P, 2, NS, BW], F32R)
        hlo = sb("hlo", [P, 2, NS, BW], F32R)
        cwb = sb("cwb", [P, 2 * HC, BW], F32)
        sg = sb("sg", [P, 2, BW], F32)
        pr = sb("pr", [P, 2, BW], F32)
        ahi = sb("ahi", [P, 2, BW], F32R)
        alo = sb("alo", [P, 2, BW], F32R)
        x1 = sb("x1b", [P, 2, TPB * D], F32)
        tok = sb("tok4", [1, 2], F32)
        hg = [ctx.enter_context(nc.psum_tensor(f"hg{i}", [P, BW], F32)) for i in range(2)]
        hu = [ctx.enter_context(nc.psum_tensor(f"hu{i}", [P, BW], F32)) for i in range(2)]
        ya = [ctx.enter_context(nc.psum_tensor(f"ya{i}", [P, NS, BW], F32)) for i in range(2)]
        names = ("h_full", "h_free", "gu_full", "silu", "dve_chain", "pr_full", "ahi_done", "act_full", "y_full",
                 "z_add", "z_full", "zt_full", "out_full", "cw_free", "x1_in0", "x1_in1", "cw_in0", "cw_in1",
                 "out_done0", "out_done1")
        q = {n: ctx.enter_context(nc.semaphore("ex_" + n)) for n in names}
        z = sb("z", [P, NS, BW], F32)

        def settle(eng, counts):
            for n, c in counts:
                eng.wait_ge(q[n], c)
            eng.drain()
            for n, c in counts:
                eng.nop().then_inc(q[n], -c)

        seq = [(p, u) for p in range(2) for u in range(U)]
        NQ = len(seq)

        with nc.Block() as block:
            @block.sync
            def _(sp):
                sp.sem_inc(q["cw_free"], 2)
                with sp.Fori(0, NB // 2) as pair:
                    b = pair * 2
                    for p in range(2):
                        sp.dma_start(x1[:, p, :], d["x1"][bass.ds(b + p, 1), :, :].rearrange("a p n -> (a p) n")
                                     ).then_inc(q[f"x1_in{p}"], 16)
                        for k in range(4):
                            sp.wait_ge(q["cw_free"], 4 * p + k + 1)
                            src = d["cw"][bass.ds(pair, 1), k * HC:(k + 1) * HC, p * BW:(p + 1) * BW]
                            sp.dma_start(cwb[:, k % 2 * HC:(k % 2 + 1) * HC, :], src.broadcast_to([P, HC, BW])
                                         ).then_inc(q[f"cw_in{k % 2}"], 16)
                    for p in range(2):
                        sp.wait_ge(q["out_full"], p + 1)
                        dst = d["out"][bass.ds((b + p) * TPB, TPB), :, :].rearrange("a p n -> p a n")
                        sp.dma_start(dst, x1[:, p, :].rearrange("p (a n) -> p a n", a=TPB)
                                     ).then_inc(q[f"out_done{p}"], 16)
                    for p in range(2):
                        sp.wait_ge(q[f"out_done{p}"], 16)
                    sp.drain()
                    for n, c in (("cw_free", 8), ("out_full", 2), ("out_done0", 16), ("out_done1", 16)):
                        sp.nop().then_inc(q[n], -c)

            @block.gpsimd
            def _(pool):
                pool.sem_inc(q["h_free"], 2)
                with pool.Fori(0, NB // 2) as pair:
                    b = pair * 2
                    for p in range(2):
                        pool.wait_ge(q["h_free"], p + 1)
                        src = h2[:, bass.ds(b + p, 1), :, :].rearrange("p a s n -> p (a s) n")
                        pool.tensor_copy(hhi[:, p, :, :], src).then_inc(q["h_full"], 1)
                        pool.drain()
                        pool.tensor_tensor(hlo[:, p, :, :], src, hhi[:, p, :, :], ALU.subtract).then_inc(q["h_full"], 1)
                    pool.drain()
                    pool.nop().then_inc(q["h_free"], -2)

            @block.tensor
            def _(pe):
                def up(n):
                    p, u = seq[n]
                    if u == 0:
                        pe.wait_ge(q["h_full"], 2 * p + 2)
                    for k, bank in ((0, hg[n % 2]), (1, hu[n % 2])):
                        m = 0
                        for s in range(NS):
                            c0 = (k * NS + s) * I
                            for w, h in ((whi, hhi), (whi, hlo), (wlo, hhi)):
                                ins = pe.matmul(bank[:, :], w[:, u, c0:c0 + I], h[:, p, s, :],
                                                start=(m == 0), stop=(m == 5))
                                m += 1
                    ins.then_inc(q["gu_full"], 1)

                def down(n):
                    p, u = seq[n]
                    pe.wait_ge(q["act_full"], n + 1)
                    for s in range(NS):
                        c0 = 2 * NS * I + s * P
                        for m, (w, a) in enumerate(((whi, ahi), (whi, alo), (wlo, ahi))):
                            ins = pe.matmul(ya[p][:, s, :], w[:, u, c0:c0 + P], a[:, n % 2, :],
                                            start=(u == 0 and m == 0), stop=(u == U - 1 and m == 2))
                    if u == U - 1:
                        ins.then_inc(q["y_full"], 1)

                def back(p):
                    pe.wait_ge(q["z_full"], 2 * p + 2)
                    out = ya[p][:, :, :].rearrange("p s (i n) -> p (s i) n", n=D)
                    for i in range(TPB):
                        for s in range(NS):
                            ins = pe.transpose(out[:, i, s * P:(s + 1) * P], z[:, s, i * P:(i + 1) * P],
                                               t["identf"][:, :])
                    ins.then_inc(q["zt_full"], 1)

                with pe.Fori(0, NB // 2):
                    for n in range(NQ):
                        up(n)
                        if n >= 1:
                            down(n - 1)
                        if n == U + 2:
                            back(0)
                    down(NQ - 1)
                    back(1)
                    settle(pe, (("h_full", 4), ("act_full", NQ), ("z_full", 4)))

            @block.scalar
            def _(act):
                def scaled(p):
                    for s in range(NS):
                        act.wait_ge(q["z_add"], 2 * p + s + 1)
                        act.activation(z[:, s, :], z[:, s, :], ACT.Copy, scale=t["gb"][:, s:s + 1]
                                       ).then_inc(q["z_full"], 1)

                def token(name):
                    act.activation(tok[:, 0:1], t["mod"][0:1, 0:1], ACT.Copy).then_inc(q[name], 1)

                def high(n):
                    act.wait_ge(q["pr_full"], n + 1)
                    act.activation(ahi[:, n % 2, :], pr[:, n % 2, :], ACT.Copy).then_inc(q["ahi_done"], 1)
                    if seq[n][1] < E and seq[n][1] % HC == HC - 1:
                        token("cw_free")

                with act.Fori(0, NB // 2):
                    for n in range(NQ):
                        act.wait_ge(q["gu_full"], n + 1)
                        act.activation(sg[:, n % 2, :], hg[n % 2][:, :], ACT.Silu).then_inc(q["silu"], 1)
                        if seq[n][1] == U - 1:
                            token("h_free")
                        high(n)
                        if n == U + 1:
                            scaled(0)
                    scaled(1)
                    settle(act, (("gu_full", NQ), ("pr_full", NQ), ("z_add", 4)))

            @block.vector
            def _(dve):
                with dve.Fori(0, NB // 2) as pair:
                    b = pair * 2
                    chain = [0]

                    def summed(p):
                        dve.wait_ge(q["y_full"], p + 1)
                        for s in range(NS):
                            dve.tensor_tensor(z[:, s, :], ya[p][:, s, :],
                                              h2[:, bass.ds(b + p, 1), s, :].rearrange("p a n -> p (a n)"), ALU.add).then_inc(q["z_add"], 1)

                    def result(p):
                        dve.wait_ge(q["zt_full"], p + 1)
                        dve.wait_ge(q[f"x1_in{p}"], 16)
                        dve.tensor_tensor(x1[:, p, :], x1[:, p, :], ya[p][:, :, :].rearrange("p s n -> p (s n)"),
                                          ALU.add).then_inc(q["out_full"], 1)

                    for n in range(NQ):
                        p, u = seq[n]
                        dve.wait_ge(q["silu"], n + 1)
                        if u < E:
                            dve.tensor_tensor(sg[:, n % 2, :], sg[:, n % 2, :], hu[n % 2][:, :],
                                              ALU.mult).then_inc(q["dve_chain"], 1)
                            chain[0] += 1
                            dve.wait_ge(q["dve_chain"], chain[0])
                            if u % HC == 0:
                                dve.wait_ge(q[f"cw_in{u // HC % 2}"], 16 * (2 * p + u // HC // 2 + 1))
                            dve.tensor_tensor(pr[:, n % 2, :], sg[:, n % 2, :], cwb[:, u % (2 * HC), :],
                                              ALU.mult).then_inc(q["pr_full"], 1)
                        else:
                            dve.tensor_tensor(pr[:, n % 2, :], sg[:, n % 2, :], hu[n % 2][:, :],
                                              ALU.mult).then_inc(q["pr_full"], 1)
                        dve.wait_ge(q["ahi_done"], n + 1)
                        dve.tensor_tensor(alo[:, n % 2, :], pr[:, n % 2, :], ahi[:, n % 2, :],
                                          ALU.subtract).then_inc(q["act_full"], 1)
                        if n == U:
                            summed(0)
                        if n == U + 4:
                            result(0)
                    summed(1)
                    result(1)
                    settle(dve, (("silu", NQ), ("dve_chain", chain[0]), ("ahi_done", NQ), ("y_full", 2),
                                 ("zt_full", 2), ("cw_in0", 64), ("cw_in1", 64), ("x1_in0", 16), ("x1_in1", 16)))


def build(nc, d):
    with ExitStack() as ctx:
        def sb(c, name, shape, dt):
            return c.enter_context(nc.sbuf_tensor(name, shape, dt))

        t = {}
        t["identf"] = sb(ctx, "identf", [P, P], F32)
        t["mod"] = sb(ctx, "mod", [P, 12], F32)
        t["gb"] = sb(ctx, "gb", [P, NS], F32)
        t["h2"] = sb(ctx, "h2", [P, NB, NS, BW], F32)
        t["y"] = t["h2"][:, :, :, :].rearrange("p b s n -> p (b s n)").rearrange("p (i n) -> p i n", n=D)
        with ExitStack() as mid:
            t["gab"] = sb(mid, "gab", [P, 2 * D], F32)
            t["x"] = sb(mid, "xres", [P, NT, D], F32)
            with ExitStack() as early:
                t["identb"] = sb(early, "identb", [P, P], BF16)
                t["maskq"] = sb(early, "maskq", [P, P], BF16)
                t["maskk"] = sb(early, "maskk", [P, P], BF16)
                t["sel"] = sb(early, "sel", [P, 32], F32)
                t["wbd"] = sb(early, "wbd", [P, 3, P], F32)
                t["v"] = sb(early, "v", [P, NT, HPAD * C], F32)
                t["vpad"] = [sb(early, f"vpad{i}", [P, NT, 32], F32) for i in range(2)]
                t["qst"] = [sb(early, f"qst{i}", [P, T], BF16) for i in range(2)]
                t["kst"] = [sb(early, f"kst{i}", [P, T], BF16) for i in range(2)]
                prepare(nc, t, d)
                attend(nc, t, d)
            for name in ("whi", "wlo"):
                t[name] = ctx.enter_context(nc.sbuf_tensor(name, [P, U, WU], F32R, side="right"))
            project(nc, t, d)
        experts(nc, t, d)


_OUT = ((1, T, D), "float32")


def kernel(**inputs):
    import numpy as _np
    import concourse.bacc as _bacc
    from concourse.bass_utils import run_bass_kernel_spmd as _run

    a = {k: _np.asarray(v) for k, v in inputs.items()}

    def units(w, s):
        both = _np.concatenate([w, s.reshape(2, I, D)], axis=0)
        return both.transpose(0, 2, 1).reshape(U, NS, P, I).transpose(0, 2, 1, 3).reshape(U, P, NS * I)

    down = _np.concatenate([a["L0_ffn_Wd"].transpose(0, 2, 1), a["L0_ffn_Ws_d"].T.reshape(2, I, D)], axis=0)
    arrays = {
        "x": a["L0_attn_x"], "c": a["L0_c"], "wmod": a["L0_wmod"], "bu": a["L0_attn_bu"],
        "WqT": a["L0_attn_Wq"].T, "WkT": a["L0_attn_Wk"].T, "WvT": a["L0_attn_Wv"].T,
        "WuT": a["L0_attn_Wu"].T, "gwT": a["L0_ffn_gate_w"].T, "gbias": a["L0_ffn_gate_bias"],
        "wcat": _np.concatenate([units(a["L0_ffn_Wg"], a["L0_ffn_Ws_g"]),
                                 units(a["L0_ffn_Wu"], a["L0_ffn_Ws_u"]), down], axis=2),
    }
    arrays = {f"in_{k}": _np.ascontiguousarray(v) for k, v in arrays.items()}
    nc = _bacc.Bacc("TRN2", target_bir_lowering=False, num_devices=1)
    d = {k[3:]: nc.dram_tensor(k, v.shape, mybir.dt.from_np(v.dtype), kind="ExternalInput").ap()
         for k, v in arrays.items()}
    for name in ("qs", "ks"):
        d[name] = nc.dram_tensor(name, [3, HPAD * C, T], BF16).ap()
    d["x1"] = nc.dram_tensor("x1", [NB, P, TPB * D], F32).ap()
    d["cw"] = nc.dram_tensor("cw", [NB // 2, E, 2 * BW], F32).ap()
    out = nc.dram_tensor("out_0", _OUT[0], mybir.dt.from_np(_np.dtype(_OUT[1])), kind="ExternalOutput").ap()
    d["out"] = out.rearrange("a (n p) c -> (a n) p c", p=P)
    build(nc, d)
    r = _run(nc, [arrays], core_ids=[0])
    return r.results[0]["out_0"]
```

```python
from contextlib import ExitStack

import concourse.bass as bass
from concourse import mybir

F32 = mybir.dt.float32
F32R = mybir.dt.float32r
BF16 = mybir.dt.bfloat16
ALU = mybir.AluOpType
ACT = mybir.ActivationFunctionType
AX_X = mybir.AxisListType.X

P = 128
T = 4096
D = 256
H = 16
C = D // H
NS = D // P
NT = T // P
BW = 512
NB = T // BW
TPB = BW // P
EPS = 1e-5
MASKED = -1e30
FLOOR = 0.25
HPAD = H + 1

QPARTS = (0, 0, 0, 1, 1, 2)
KPARTS = (0, 1, 2, 0, 1, 0)
ROWS = C * len(QPARTS)
SROWS = ROWS + 2

E = 16
TOPK = 4
NG = 4
TG = 2
RSCALE = 2.5
I = 128
U = E + 2
WU = 2 * NS * I + D

LEAD = 5
SW = 1
S_SLOTS = 3
ST_SLOTS = 3
M_SLOTS = 4


def slot_constants(pool, t, i):
    yield pool.memset(t["vpad"][i][:, :, C:32], 0.0)
    yield pool.memset(t["vpad"][i][:, :, C:C + 1], 1.0)
    yield pool.memset(t["kst"][i][ROWS:P, :], 1.0)
    yield pool.memset(t["qst"][i][ROWS:P, :], 0.0)


def prepare(nc, t, d):
    with ExitStack() as ctx:
        def sb(name, shape, dt):
            return ctx.enter_context(nc.sbuf_tensor(name, shape, dt))

        def sem(name):
            return ctx.enter_context(nc.semaphore(name))

        QKR = 4
        PR = 8
        wmod = sb("wmod", [P, NS, 6 * D], F32)
        ccol = sb("ccol", [P, NS], F32)
        scol = sb("scol", [P, NS], F32)
        wrep = sb("wrep", [P, 3, C], F32)
        onb = sb("onb", [P, P // C, C], F32)
        wbd = t["wbd"]
        hT = t["h2"]
        xn = sb("xn", [P, 2, TPB, D], F32)
        stats = sb("stats", [P, NT, 6], F32)
        mv = sb("mv", [P, NT, 2], F32)
        ve = sb("ve", [P, NT], F32)
        rstd = sb("rstd", [P, NT], F32)
        half = sb("half", [P, NT], F32)
        grow = sb("grow", [1, 2 * D], F32)
        gtmp = sb("gtmp", [1, 3, D], F32)
        burow = sb("burow", [1, D], F32)
        gbt = sb("gbt", [P, 3, NS], F32)
        ones1 = sb("ones1", [1, P], F32)
        parts = sb("parts", [P, PR, 3, BW], BF16)
        rest = sb("rest", [P, QKR, BW], F32)
        tp = [ctx.enter_context(nc.psum_tensor(f"tp{i}", [P, BW], F32)) for i in range(2)]
        qk = [ctx.enter_context(nc.psum_tensor(f"qk{i}", [P, BW], F32)) for i in range(QKR)]
        modp = ctx.enter_context(nc.psum_tensor("modp", [P, BW], F32))

        s_c, s_wm, s_wr, s_bu = sem("c_in"), sem("wmod_in"), sem("wrep_in"), sem("bu_in")
        s_wm2 = sem("wmod_rest_in")
        s_x = [sem(f"x_in{g}") for g in range(4)]
        s_store = [sem(f"parts_out{i}") for i in range(PR)]
        s_zero = sem("zero_rows_out")
        s_pool, s_const, s_dve = sem("pool_chain"), sem("constants"), sem("dve_chain")
        s_silu, s_modp, s_mod = sem("silu_c"), sem("mod_psum"), sem("mod_ready")
        s_grow, s_bc, s_ve, s_rstd, s_xn = sem("ga_row"), sem("ga_bcast"), sem("ve"), sem("rstd"), sem("xn")
        s_tp, s_hT, s_wbd = sem("transposed"), sem("hT_ready"), sem("wbd_ready")
        s_qk, s_p1, s_r, s_p2, s_p3 = sem("qk_psum"), sem("part1"), sem("rest"), sem("part2"), sem("part3")
        GT = NT // 4
        chunks = [(b, s, w) for b in range(NB) for s in range(NS) for w in range(2)]

        with nc.Block() as block:
            @block.sync
            def _(sp):
                xv = d["x"].rearrange("a (n p) c -> p (a n) c", p=P)
                sp.dma_start(ccol[:, :], d["c"].rearrange("a (s p) -> p (a s)", p=P),
                             allow_slow_non_contiguous=True).then_inc(s_c, 16)

                def load_x(g):
                    sp.dma_start(t["x"][:, g * GT:(g + 1) * GT, :], xv[:, g * GT:(g + 1) * GT, :]).then_inc(s_x[g], 16)

                wm = d["wmod"].rearrange("(s p) n -> p s n", p=P)
                sp.dma_start(wmod[:, :, 0:2 * D], wm[:, :, 0:2 * D]).then_inc(s_wm, 16)
                load_x(0)
                sp.dma_start(wmod[:, :, 2 * D:6 * D], wm[:, :, 2 * D:6 * D]).then_inc(s_wm2, 16)
                for g in range(1, 4):
                    load_x(g)
                sp.wait_ge(s_const, 2)
                for which in ("qs", "ks"):
                    for k in range(3):
                        sp.dma_start(d[which][k, D:HPAD * C, :], t["qst"][0][0:C, :]).then_inc(s_zero, 16)
                for c, (b, s, w) in enumerate(chunks):
                    sp.wait_ge(s_p3, c + 1)
                    dst = d["ks" if w else "qs"][:, s * P:(s + 1) * P, b * BW:(b + 1) * BW]
                    sp.dma_start(dst.rearrange("k p n -> p k n"), parts[:, c % PR, :, :]).then_inc(s_store[c % PR], 16)
                for i in range(PR):
                    sp.wait_ge(s_store[i], 16 * len(chunks) // PR)
                sp.wait_ge(s_zero, 96)

            @block.gpsimd
            def _(pool):
                n = [0]

                def link(ins):
                    n[0] += 1
                    ins.then_inc(s_pool, 1)
                    pool.wait_ge(s_pool, n[0])

                link(pool.memset(t["identf"][:, :], 0.0))
                link(pool.affine_select(out=t["identf"][:, :], in_=t["identf"][:, :], compare_op=ALU.not_equal,
                                        fill=1.0, base=0, pattern=[[-1, P]], channel_multiplier=1))
                link(pool.memset(onb[:, :, :], 1.0))
                link(pool.affine_select(out=onb[:, :, :], in_=onb[:, :, :], compare_op=ALU.is_ge, fill=0.0,
                                        base=0, pattern=[[-C, P // C], [0, C]], channel_multiplier=1))
                link(pool.affine_select(out=onb[:, :, :], in_=onb[:, :, :], compare_op=ALU.is_ge, fill=0.0,
                                        base=C - 1, pattern=[[C, P // C], [0, C]], channel_multiplier=-1))
                link(pool.memset(ones1[:, :], 1.0))
                link(pool.memset(t["maskq"][:, :], 0.0))
                link(pool.affine_select(out=t["maskq"][:, :], in_=t["maskq"][:, :], compare_op=ALU.is_ge,
                                        fill=MASKED, base=0, pattern=[[-1, P]], channel_multiplier=1))
                link(pool.memset(t["maskk"][:, :], 0.0))
                link(pool.affine_select(out=t["maskk"][:, :], in_=t["maskk"][:, :], compare_op=ALU.is_ge,
                                        fill=MASKED, base=0, pattern=[[1, P]], channel_multiplier=-1))
                pool.memset(half[:, :], -0.5).then_inc(s_const, 1)
                pool.wait_ge(s_const, 1)

                def power(g):
                    pool.wait_ge(s_ve, g + 1)
                    c0, c1 = g * GT, (g + 1) * GT
                    pool.tensor_tensor(rstd[:, c0:c1], ve[:, c0:c1], half[:, c0:c1], ALU.pow).then_inc(s_rstd, 1)

                power(0)
                link(pool.memset(t["qst"][0][0:C, :], 0.0))
                pool.memset(t["v"][:, :, D:HPAD * C], 0.0).then_inc(s_const, 1)
                power(1)
                for slot in slot_constants(pool, t, 0):
                    link(slot)
                for c, (b, s, w) in enumerate(chunks):
                    pool.wait_ge(s_p2, c + 1)
                    i = c % QKR
                    pool.tensor_tensor(parts[:, c % PR, 2, :], rest[:, i, :], parts[:, c % PR, 1, :],
                                       ALU.subtract).then_inc(s_p3, 1)
                    if c % 4 == 3 and b % 2 == 0 and b // 2 + 2 < 4:
                        power(b // 2 + 2)

            @block.vector
            def _(dve):
                n = [0]

                def link(ins):
                    n[0] += 1
                    ins.then_inc(s_dve, 1)
                    dve.wait_ge(s_dve, n[0])

                dve.wait_ge(s_const, 1)
                link(dve.tensor_copy(t["identb"][:, :], t["identf"][:, :]))
                dve.wait_ge(s_wr, 16)
                scale = float(D) ** -0.25
                for w in range(3):
                    ins = dve.scalar_tensor_tensor(
                        out=wbd[:, w, :].rearrange("p (h o) -> p h o", o=C), in0=onb[:, :, :],
                        scalar=scale if w < 2 else 1.0, in1=wrep[:, w, :].unsqueeze(1).broadcast_to([P, P // C, C]),
                        op0=ALU.mult, op1=ALU.mult)
                ins.then_inc(s_wbd, 1)

                def modulation():
                    dve.wait_ge(s_modp, 1)
                    link(dve.tensor_copy(t["mod"][:, 0:4], modp[:, 0:4]))
                    dve.tensor_scalar(t["mod"][:, 2:4], t["mod"][:, 2:4], 1.0, None, ALU.add).then_inc(s_mod, 1)

                def gates():
                    dve.wait_ge(s_modp, 2)
                    link(dve.tensor_copy(t["mod"][:, 4:12], modp[:, 4:12]))
                    dve.tensor_scalar(t["mod"][:, 8:10], t["mod"][:, 8:10], 1.0, None, ALU.add)
                    floor_gate(t["mod"][:, 10:12], gbt)
                    link(dve.tensor_copy(t["gb"][:, :], gbt[:, 0, :]))
                    link(dve.tensor_copy(gtmp[:, 0, :], modp[0:1, 16:16 + D]))
                    floor_gate(gtmp[:, 0, :], gtmp)
                    link(dve.tensor_copy(grow[:, 0:D], gtmp[:, 0, :]))
                    dve.wait_ge(s_bu, 16)
                    dve.tensor_tensor(grow[:, D:2 * D], gtmp[:, 0, :], burow[:, :], ALU.mult).then_inc(s_mod, 1)

                def floor_gate(src, b):
                    link(dve.tensor_scalar(b[:, 1, :], src, -1.0, None, ALU.mult))
                    link(dve.tensor_tensor(b[:, 1, :], b[:, 1, :], src, ALU.max))
                    link(dve.tensor_scalar(b[:, 2, :], src, 0.0, 2.0, ALU.is_ge, ALU.mult))
                    link(dve.tensor_scalar(b[:, 2, :], b[:, 2, :], -1.0, None, ALU.add))
                    link(dve.tensor_scalar(b[:, 1, :], b[:, 1, :], FLOOR, None, ALU.max))
                    link(dve.tensor_tensor(b[:, 0, :], b[:, 1, :], b[:, 2, :], ALU.mult))

                def statistics(g):
                    dve.wait_ge(s_x[g], 16)
                    ts = range(g * GT, (g + 1) * GT)
                    for i in ts:
                        ins = dve.bn_stats(stats[:, i, :], t["x"][:, i, :])
                    link(ins)
                    for i in ts:
                        ins = dve.bn_aggr(mv[:, i, :], stats[:, i, :])
                    link(ins)
                    dve.tensor_scalar(ve[:, ts[0]:ts[-1] + 1], mv[:, ts[0]:ts[-1] + 1, 1], EPS, None,
                                      ALU.add).then_inc(s_ve, 1)

                def normalised(b):
                    dve.wait_ge(s_rstd, b // 2 + 1)
                    if b >= 2:
                        dve.wait_ge(s_tp, NS * (b - 1))
                    for i in range(TPB * b, TPB * (b + 1)):
                        dve.tensor_scalar(xn[:, b % 2, i % TPB, :], t["x"][:, i, :], mv[:, i, 0:1], rstd[:, i:i + 1],
                                          ALU.subtract, ALU.mult).then_inc(s_xn, 1)

                def rests(b):
                    for c in range(4 * b, 4 * b + 4):
                        i = c % QKR
                        dve.wait_ge(s_p1, c + 1)
                        if c >= QKR:
                            dve.wait_ge(s_p3, c - QKR + 1)
                        dve.tensor_tensor(rest[:, i, :], qk[i][:, :], parts[:, c % PR, 0, :],
                                          ALU.subtract).then_inc(s_r, 1)

                modulation()
                statistics(0)
                normalised(0)
                statistics(1)
                normalised(1)
                gates()
                for b in range(NB):
                    if b % 2 == 0 and b // 2 + 2 < 4:
                        statistics(b // 2 + 2)
                    if b + 2 < NB:
                        normalised(b + 2)
                    rests(b)
                dve.wait_ge(s_bc, 1)
                dve.tensor_copy(t["gab"][:, :], modp[:, :])

            @block.scalar
            def _(act):
                act.dma_start(wrep[:, :, :], d["wrep"]).then_inc(s_wr, 16)
                act.dma_start(burow[:, :], d["bu"].rearrange("(a n) -> a n", a=1)).then_inc(s_bu, 16)
                act.wait_ge(s_c, 16)
                act.activation(scol[:, :], ccol[:, :], ACT.Silu).then_inc(s_silu, 1)
                act.wait_ge(s_mod, 1)

                def modulated(b):
                    for s in range(NS):
                        act.wait_ge(s_tp, NS * b + s + 1)
                        act.activation(hT[:, b, s, :], tp[s][:, :], ACT.Identity,
                                       scale=t["mod"][:, 2 + s:3 + s], bias=t["mod"][:, s:s + 1]).then_inc(s_hT, 1)

                def part2(c):
                    act.wait_ge(s_r, c + 1)
                    act.activation(parts[:, c % PR, 1, :], rest[:, c % QKR, :], ACT.Copy).then_inc(s_p2, 1)

                modulated(0)
                for c, (b, s, w) in enumerate(chunks):
                    i = c % QKR
                    if c % 4 == 0 and b + 1 < NB:
                        modulated(b + 1)
                    act.wait_ge(s_qk, c + 1)
                    if c >= PR:
                        act.wait_ge(s_store[c % PR], 16 * (c // PR))
                    act.activation(parts[:, c % PR, 0, :], qk[i][:, :], ACT.Copy).then_inc(s_p1, 1)
                    if c >= 1:
                        part2(c - 1)
                part2(len(chunks) - 1)

            @block.tensor
            def _(pe):
                def columns(j0, j1):
                    for j in range(j0, j1):
                        for s in range(NS):
                            ins = pe.matmul(modp[:, j:j + 1], wmod[:, s, j * P:(j + 1) * P], scol[:, s:s + 1],
                                            start=(s == 0), stop=(s == NS - 1))
                    return ins

                pe.wait_ge(s_silu, 1)
                pe.wait_ge(s_wm, 16)
                columns(0, 4).then_inc(s_modp, 1)
                pe.wait_ge(s_const, 1)
                pe.wait_ge(s_wbd, 1)

                def turn(b):
                    pe.wait_ge(s_xn, TPB * (b + 1))
                    for s in range(NS):
                        if b:
                            pe.wait_ge(s_hT, NS * (b - 1) + s + 1)
                        for i in range(TPB):
                            ins = pe.transpose(tp[s][:, i * P:(i + 1) * P],
                                               xn[:, b % 2, i, s * P:(s + 1) * P], t["identf"][:, :])
                        ins.then_inc(s_tp, 1)

                turn(0)
                pe.wait_ge(s_wm2, 16)
                pe.wait_ge(s_mod, 1)
                columns(4, 12)
                for s in range(NS):
                    ins = pe.matmul(modp[0:1, 16:16 + D], scol[:, s:s + 1], wmod[:, s, 2 * D:3 * D],
                                    start=(s == 0), stop=(s == NS - 1))
                ins.then_inc(s_modp, 1)
                for c, (b, s, w) in enumerate(chunks):
                    if c % 4 == 0:
                        if b + 1 < NB:
                            turn(b + 1)
                        pe.wait_ge(s_hT, 2 * b + 2)
                    if c >= QKR:
                        pe.wait_ge(s_r, c - QKR + 1)
                    pe.matmul(qk[c % QKR][:, :], wbd[:, w, :], hT[:, b, s, :],
                              start=True, stop=True).then_inc(s_qk, 1)
                pe.wait_ge(s_mod, 2)
                pe.matmul(modp[:, :], ones1[:, :], grow[:, :], start=True, stop=True).then_inc(s_bc, 1)


PV_LAG, YO_LAG, MT_LAG = 6, 7, 8
UNITS = [(slot, j, k) for slot in (0, 1) for j in range(NB) for k in range(TPB * (j + 1))]
NU = len(UNITS)
WRAP = 13


def tile_jobs(slot, j):
    jobs = []
    for r in range(TPB):
        keys = (TPB * j + r + 1) * P
        for c in range(-(-keys // (SW * BW))):
            jobs.append((slot, j, r, c, c * SW * BW, min(keys, (c + 1) * SW * BW)))
    return [(x, i == len(jobs) - 1) for i, x in enumerate(jobs)]


def schedule():
    ahead = [job for j in range(LEAD) for job in tile_jobs(0, j)]
    pair = [job for slot, j in [(0, j) for j in range(LEAD, NB)] + [(1, j) for j in range(NB)] +
            [(0, j) for j in range(LEAD)] for job in tile_jobs(slot, j)]
    cost = [x[5] - x[4] + 200 for x, _ in pair]
    events, later, sent = [], [], 0

    def maxima(job, at):
        nonlocal later, sent
        x, last = job
        if last:
            due = [e for _, e in later if e[0] == "MT"][:-(M_SLOTS - 2)]
            events.extend(due)
            later = [(w, e) for w, e in later if e not in due]
        events.append(("S", (sent, x, last)))
        sent += 1
        if last:
            later.append((at + MT_LAG, ("MT", (x[0], x[1]))))

    first = NT // 4
    events += [("VP", i) for i in range(first)]
    begin = [i for i, (x, last) in enumerate(ahead) if last][2] + 1
    every = begin // (NT // 2 - first)
    for i in range(begin):
        maxima(ahead[i], -MT_LAG)
        if i % every == every - 1:
            events.append(("VP", first + i // every))
    assert begin // every >= NT // 2 - first
    events.append(("V", 0))
    done = begin
    cut, spent, n = 0, 0, 0
    for s in range(NU + WRAP):
        if s == WRAP:
            cut = len(events)
        if s == NU:
            assert n == len(pair)
            spent, n = 0, 0
        events += [e for at, e in later if at == s]
        later = [(at, e) for at, e in later if at != s]
        slot, j, k = UNITS[s % NU]
        early = [e for _, e in later if k == 0 and e == ("MT", (slot, j))]
        events += early
        later = [(at, e) for at, e in later if e not in early]
        events.append(("ST", (s, slot, j, k)))
        if k == TPB * NB - 1:
            later.append((s + 3, ("FREE", slot)))
        if k == 3 and j == 3:
            later.append((s + 1, ("V", 1 - slot)))
        if s >= WRAP and (s - WRAP) % (NU // 4) == 0:
            events.append(("X", (s - WRAP) // (NU // 4)))
        g = s - PV_LAG
        if g >= 0 and g % TPB == 0:
            slot, j, k = UNITS[g % NU]
            events.append(("PV", (g // TPB, slot, j, k // TPB)))
            if k // TPB == j:
                later += [(s + 1, ("OD", (slot, j))), (s + 1 + YO_LAG, ("YO", (slot, j)))]
        while done < len(ahead) and done - begin < (len(ahead) - begin) * (s + 1) / (WRAP - 2):
            maxima(ahead[done], s + 1 - MT_LAG)
            done += 1
        while done == len(ahead) and n < len(pair) and spent <= sum(cost) * (s % NU + 1) / NU:
            maxima(pair[n], s)
            spent += cost[n]
            n += 1
    assert not [e for e in events[:cut] if e[0] in ("YO", "FREE")]
    return events[:cut], events[cut:]


class Ledger:

    def __init__(self, eng, sems):
        self.eng, self.sems = eng, sems
        self.n, self.seen, self.base = {}, {}, {}

    def raised(self, name, by=1):
        self.n[name] = self.n.get(name, 0) + by
        return self.n[name]

    def wait(self, name, mark=None):
        mark = self.n.get(name, 0) if mark is None else mark
        if mark > self.seen.get(name, 0):
            self.seen[name] = mark
            self.eng.wait_ge(self.sems[name], mark - self.base.get(name, 0))

    def settle(self):
        self.eng.drain()
        for name in sorted(self.seen):
            by = self.seen[name] - self.base.get(name, 0)
            if by:
                self.eng.nop().then_inc(self.sems[name], -by)
            self.base[name] = self.seen[name]

    def ahead(self):
        return {name: n - self.base.get(name, 0) for name, n in self.n.items()}

    def run(self, section, prologue, turn, turns, epilogue=(), over=()):
        def part(events, n):
            section(events, n)
            for name in over:
                self.wait(name)
            self.settle()

        part(prologue, 0)
        before = self.ahead()
        with self.eng.Fori(0, turns) as n:
            part(turn, n)
        after = self.ahead()
        assert all(after[k] == before.get(k, 0) for k in after), (before, after)
        if epilogue:
            part(epilogue, turns)


def attend(nc, t, d):
    with ExitStack() as ctx:
        def sb(name, shape, dt):
            return ctx.enter_context(nc.sbuf_tensor(name, shape, dt))

        NP = 16
        prob = sb("prob", [P, NP, BW], F32)
        mx = sb("mx", [P, M_SLOTS, TPB, NB // SW], F32)
        mq = sb("mq", [P, M_SLOTS, TPB], F32)
        nm = sb("nm", [P, M_SLOTS, TPB], F32)
        mt = sb("mt", [P, M_SLOTS, TPB, 2], BF16)
        od = sb("od", [P, 2, BW], F32)
        ys = sb("ys", [P, 2, TPB, C + 1], F32)
        rl = sb("rl", [P, 2, TPB], F32)
        tok = sb("tok", [1, 2], F32)
        S = [ctx.enter_context(nc.psum_tensor(f"S{i}", [P, SW * BW], F32)) for i in range(S_SLOTS)]
        ST = [ctx.enter_context(nc.psum_tensor(f"ST{i}", [P, BW], F32)) for i in range(ST_SLOTS)]
        O = ctx.enter_context(nc.psum_tensor("O", [P, BW], F32))
        M = ctx.enter_context(nc.psum_tensor("M", [P, BW], F32))
        names = ("s_full", "s_read", "s_last_read", "st_full", "exp_done", "pv_done", "od_done", "m_full",
                 "m_split", "mt_full", "m_copied", "y_full", "y_done", "v_full", "dve_chain", "pool_chain",
                 "heads_free", "stack0", "stack1", "y_chain")
        q = {n: ctx.enter_context(nc.semaphore("at_" + n)) for n in names}
        s_vp, s_vc, s_slot = (ctx.enter_context(nc.semaphore(n)) for n in ("vp_full", "v_copied", "slot_ready"))
        qst, kst, vpad = t["qst"], t["kst"], t["vpad"]

        prologue, turn = schedule()

        def run(eng, section, over=()):
            led = Ledger(eng, q)
            led.run(lambda events, pair: section(events, led, pair * 2), prologue, turn, H // 2, over=over)

        LOADED = 16 * (len(QPARTS) + len(KPARTS))

        def load(sp, slot, head):
            row = head * C
            for name, st, parts in (("qs", qst[slot], QPARTS), ("ks", kst[slot], KPARTS)):
                for i, k in enumerate(parts):
                    sp.dma_start(st[i * C:(i + 1) * C, :], d[name][k, bass.ds(row, C), :]
                                 ).then_inc(q[f"stack{slot}"], 16)

        with nc.Block() as block:
            @block.sync
            def _(sp):
                load(sp, 0, 0)
                sp.sem_inc(q["heads_free"], 1)
                with sp.Fori(0, H // 2) as pair:
                    h = pair * 2
                    for n, slot in enumerate((1, 0)):
                        sp.wait_ge(q["heads_free"], n + 1)
                        load(sp, slot, h + 1 + n)
                    sp.drain()
                    sp.nop().then_inc(q["heads_free"], -2)

            @block.tensor
            def _(pe):
                read = []
                mrow = {}

                def section(events, led, _):
                    for kind, e in events:
                        if kind == "S":
                            n, (slot, j, r, c, k0, k1), last = e
                            if j == 0 and r == 0:
                                led.raised(f"stack{slot}", LOADED)
                                led.wait(f"stack{slot}")
                            if n >= S_SLOTS:
                                led.wait(*read[n - S_SLOTS])
                            src = "s_last_read" if last else "s_read"
                            read.append((src, led.raised(src)))
                            qc = (TPB * j + r) * P
                            for a in range(k0, k1, BW):
                                b = min(a + BW, k1)
                                diag = b == qc + P
                                ins = pe.matmul(S[n % S_SLOTS][:, a - k0:b - k0], qst[slot][0:ROWS, qc:qc + P],
                                                kst[slot][0:ROWS, a:b], start=True, stop=not diag)
                                if diag:
                                    ins = pe.matmul(S[n % S_SLOTS][:, b - P - k0:b - k0], t["identb"][:, :],
                                                    t["maskq"][:, :], start=False, stop=True)
                            ins.then_inc(q["s_full"], 1)
                        elif kind == "VP":
                            if e >= ST_SLOTS:
                                pe.wait_ge(s_vc, e - ST_SLOTS + 1)
                            for i in range(2):
                                n = 2 * e + i
                                for s in range(NS):
                                    ins = pe.matmul(ST[e % ST_SLOTS][:, i * D + s * P:i * D + (s + 1) * P],
                                                    t["h2"][:, n // TPB, s, n % TPB * P:(n % TPB + 1) * P],
                                                    t["wbd"][:, 2, :], start=True, stop=True)
                            ins.then_inc(s_vp, 1)
                        elif kind == "MT":
                            slot, j = e
                            led.raised("mt_full")
                            led.wait("mt_full")
                            led.wait("m_copied")
                            led.wait("y_done")
                            for i in range(TPB):
                                ins = pe.matmul(M[ROWS:SROWS, i * P:(i + 1) * P], mt[:, j % M_SLOTS, i, :],
                                                t["identb"][:, :], start=True, stop=True)
                            ins.then_inc(q["m_split"], 1)
                            mrow[e] = led.raised("m_copied")
                        elif kind == "ST":
                            s, slot, j, k = e
                            if k == 0:
                                led.wait("m_copied", mrow[(slot, j)])
                            if s == 0:
                                pe.wait_ge(s_vc, NT // 2)
                            led.wait("exp_done", s - ST_SLOTS + 1)
                            c0 = max(0, k - TPB * j) * P
                            diag = k >= TPB * j
                            q0 = j * BW
                            ins = pe.matmul(ST[s % ST_SLOTS][:, c0:BW], kst[slot][0:SROWS, k * P:(k + 1) * P],
                                            qst[slot][0:SROWS, q0 + c0:q0 + BW], start=True, stop=not diag)
                            if diag:
                                ins = pe.matmul(ST[s % ST_SLOTS][:, c0:c0 + P], t["identb"][:, :],
                                                t["maskk"][:, :], start=False, stop=True)
                            ins.then_inc(q["st_full"], 1)
                            led.raised("exp_done")
                        elif kind == "PV":
                            g, slot, j, G = e
                            if G == 0:
                                led.wait("od_done")
                                if j == 0:
                                    led.raised("v_full")
                                    led.wait("v_full")
                            led.wait("exp_done", TPB * (g + 1))
                            for r in range(TPB):
                                k = TPB * G + r
                                c0 = r * P if G == j else 0
                                row = 32 * r if j else 0
                                ins = pe.matmul(O[row:row + 32, c0:BW], vpad[slot][:, k, :],
                                                prob[:, (TPB * g + r) % NP, c0:BW],
                                                start=(G == 0 if j else r == 0),
                                                stop=(G == j if j else r == 3), tile_position=(0, row),
                                                skip_group_check=True)
                            ins.then_inc(q["pv_done"], 1)
                            if G == j:
                                led.raised("od_done")
                        elif kind == "YO":
                            slot, j = e
                            led.wait("od_done")
                            led.wait("m_copied")
                            led.wait("y_done")
                            rows = P if j else 32
                            for i in range(TPB):
                                ins = pe.transpose(M[:, i * P:i * P + rows], od[0:rows, j % 2, i * P:(i + 1) * P],
                                                   t["identf"][0:rows, 0:rows])
                            ins.then_inc(q["y_full"], 1)
                            led.raised("y_done")

                run(pe, section, over=("m_copied", "y_done"))

            @block.scalar
            def _(act):
                def vcopy(slot, head):
                    act.activation(vpad[slot][:, :, 0:C], t["v"][:, :, bass.ds(head * C, C)],
                                   ACT.Copy).then_inc(q["v_full"], 1)

                def section(events, led, h):
                    for kind, e in events:
                        if kind == "VP":
                            act.wait_ge(s_vp, e + 1)
                            act.activation(t["v"][:, 2 * e:2 * e + 2, 0:D],
                                           ST[e % ST_SLOTS][:, :].rearrange("p (a n) -> p a n", a=2),
                                           ACT.Copy).then_inc(s_vc, 1)
                        elif kind == "MT":
                            slot, j = e
                            led.raised("m_split")
                            led.wait("m_split")
                            act.activation(qst[slot][ROWS:SROWS, j * BW:(j + 1) * BW], M[ROWS:SROWS, :],
                                           ACT.Copy).then_inc(q["m_copied"], 1)
                        elif kind == "ST":
                            s, slot, j, k = e
                            led.raised("st_full")
                            led.wait("st_full")
                            if s % TPB == 0:
                                led.wait("pv_done", (s - NP) // TPB + 1)
                            c0 = max(0, k - TPB * j) * P
                            act.activation(prob[:, s % NP, c0:BW], ST[s % ST_SLOTS][:, c0:BW],
                                           ACT.Exp).then_inc(q["exp_done"], 1)
                        elif kind == "PV":
                            led.raised("pv_done")
                        elif kind == "OD":
                            slot, j = e
                            led.wait("pv_done")
                            rows = P if j else 32
                            act.activation(od[0:rows, j % 2, :], O[0:rows, :], ACT.Copy).then_inc(q["od_done"], 1)
                        elif kind == "V":
                            if events is prologue:
                                act.wait_ge(s_vc, NT // 2)
                                vcopy(0, 0)
                            else:
                                vcopy(e, h + (1 if e else 2))
                        elif kind == "FREE":
                            act.activation(tok[:, 0:1], t["mod"][0:1, 0:1], ACT.Copy).then_inc(q["heads_free"], 1)

                run(act, section)

            @block.vector
            def _(dve):
                def section(events, led, h):
                    for kind, e in events:
                        if kind == "S":
                            n, (slot, j, r, c, k0, k1), last = e
                            led.raised("s_full")
                            led.wait("s_full")
                            ins = dve.tensor_reduce(mx[:, j % M_SLOTS, r, c:c + 1], S[n % S_SLOTS][:, 0:k1 - k0],
                                                    AX_X, ALU.max)
                            if not last:
                                ins.then_inc(q["s_read"], 1)
                                continue
                            ins.then_inc(q["dve_chain"], 1)
                            led.raised("dve_chain")
                            led.wait("dve_chain")
                            dve.tensor_reduce(mq[:, j % M_SLOTS, :], mx[:, j % M_SLOTS, :, 0:c + 1], AX_X,
                                              ALU.max).then_inc(q["m_full"], 1)
                        elif kind == "YO":
                            slot, j = e
                            led.raised("y_full")
                            led.wait("y_full")
                            y = ys[:, j % 2, :, :]
                            if j:
                                part = M[:, :].rearrange("p (a r c) -> p a c r", a=TPB, r=4)[:, :, 0:C + 1, :]
                                dve.tensor_reduce(y, part, AX_X, ALU.add).then_inc(q["y_chain"], 1)
                            else:
                                part = M[:, :].rearrange("p (a c) -> p a c", a=TPB)[:, :, 0:C + 1]
                                dve.tensor_copy(y, part).then_inc(q["y_chain"], 1)
                            led.raised("y_chain")
                            led.wait("y_chain")
                            dve.reciprocal(rl[:, j % 2, :], y[:, :, C]).then_inc(q["y_chain"], 1)
                            led.raised("y_chain")
                            led.wait("y_chain")
                            dve.tensor_tensor(
                                t["y"][:, TPB * j:TPB * j + TPB, bass.ds((h + slot) * C, C)], y[:, :, 0:C],
                                rl[:, j % 2, :].unsqueeze(2).broadcast_to([P, TPB, C]),
                                ALU.mult).then_inc(q["y_done"], 1)

                run(dve, section)

            @block.gpsimd
            def _(pool):
                def section(events, led, h):
                    for kind, e in events:
                        if kind == "X":
                            x = t["x"][:, bass.ds(h * 2 + e, 1), :].rearrange("p a n -> p (a n)")
                            pool.tensor_tensor(x, x, t["gab"][:, D:2 * D], ALU.add)
                        elif kind == "S" and e[2]:
                            j = e[1][1] % M_SLOTS
                            led.raised("m_full")
                            led.wait("m_full")
                            pool.tensor_scalar(nm[:, j, :], mq[:, j, :], -1.0, None,
                                               ALU.mult).then_inc(q["s_last_read"], 1)
                            pool.tensor_scalar(mt[:, j, :, 0], mq[:, j, :], -1.0, None,
                                               ALU.mult).then_inc(q["pool_chain"], 1)
                            led.raised("pool_chain")
                            led.wait("pool_chain")
                            pool.tensor_tensor(mt[:, j, :, 1], nm[:, j, :], mt[:, j, :, 0],
                                               ALU.subtract).then_inc(q["mt_full"], 1)

                for n, ins in enumerate(slot_constants(pool, t, 1)):
                    ins.then_inc(s_slot, 1)
                    pool.wait_ge(s_slot, n + 1)
                run(pool, section)


def project(nc, t, d):
    with ExitStack() as ctx:
        def sb(name, shape, dt):
            return ctx.enter_context(nc.sbuf_tensor(name, shape, dt))

        def sem(name):
            return ctx.enter_context(nc.semaphore(name))

        WR = 3
        QT = 2 * TPB
        cuts = [[u for u in range(U) if u * NB // U == b] for b in range(NB)]
        wraw = sb("wraw", [P, WR, WU], F32)
        wu = sb("wu", [P, NS, D], F32)
        gwT = sb("gwT", [P, NS, E], F32)
        bias = sb("bias", [P, E], F32)
        yT = sb("yT", [P, NS, BW], F32)
        xn = sb("xn2", [P, 2, TPB, D], F32)
        stats = sb("stats2", [P, 2, TPB, 6], F32)
        mv = sb("mv2", [P, 2, TPB, 2], F32)
        ve = sb("ve2", [P, 2, TPB], F32)
        rstd = sb("rstd2", [P, 2, TPB], F32)
        half = sb("half2", [P, TPB], F32)
        sc = sb("sc", [P, NT, E], F32)
        sfc = sb("sfc", [P, QT, E], F32)
        left = sb("left", [P, QT, E], F32)
        gs = sb("gs", [P, QT, NG], F32)
        grank = sb("grank", [P, QT, NG], F32)
        gtmp = sb("gtmp2", [P, QT, NG], F32)
        top = sb("top", [P, QT, 8], F32)
        wsum = sb("wsum", [P, QT], F32)
        cwe = sb("cwe", [P, 4, P], F32)
        cwT = sb("cwT", [P, 4, P], F32)
        tpy = [ctx.enter_context(nc.psum_tensor(f"tpy{i}", [P, BW], F32)) for i in range(2)]
        pj = [ctx.enter_context(nc.psum_tensor(f"pj{i}", [P, BW], F32)) for i in range(2)]
        tpx = [ctx.enter_context(nc.psum_tensor(f"tpx{i}", [P, BW], F32)) for i in range(2)]
        gl = [ctx.enter_context(nc.psum_tensor(f"gl{i}", [P, 2, P], F32)) for i in range(2)]

        s_w = [sem(f"wraw_in{i}") for i in range(WR)]
        s_wu, s_gw, s_bias, s_x1, s_cwo = sem("wu_in"), sem("gw_in"), sem("bias_in"), sem("x1_out"), sem("cw_out")
        s_hi, s_dve, s_cut, s_half = sem("high_parts"), sem("dve_chain2"), sem("cut"), sem("half_ready")
        s_tpy, s_yT, s_wus, s_pj, s_x1r = sem("tpy"), sem("yT_ready"), sem("wu_scaled"), sem("pj"), sem("x1_ready")
        s_ve, s_rstd, s_xn, s_tpx, s_h2 = sem("ve_ready"), sem("rstd_ready"), sem("xn_ready"), sem("tpx"), sem("h2_ready")
        s_gl, s_sig, s_cw, s_tpc, s_cwT = sem("gl"), sem("sigmoid"), sem("cw_ready"), sem("tpc"), sem("cwT_ready")
        whi, wlo = t["whi"], t["wlo"]

        STEPS = NB + 5

        with nc.Block() as block:
            @block.sync
            def _(sp):
                for u in range(U):
                    if u >= WR:
                        sp.wait_ge(s_cut, u - WR + 1)
                    sp.dma_start(wraw[:, u % WR, :], d["wcat"][u]).then_inc(s_w[u % WR], 16)

            @block.scalar
            def _(act):
                act.dma_start(wu[:, :, :], d["WuT"].rearrange("(s p) n -> p s n", p=P)).then_inc(s_wu, 16)
                act.dma_start(gwT[:, :, :], d["gwT"].rearrange("(s p) n -> p s n", p=P)).then_inc(s_gw, 16)
                act.dma_start(bias[:, :], d["gbias"].unsqueeze(0).broadcast_to([P, E])).then_inc(s_bias, 16)

                def turned(b):
                    if b >= 1:
                        act.wait_ge(s_pj, 2 * b)
                    for s in range(NS):
                        act.wait_ge(s_tpy, NS * b + s + 1)
                        act.activation(yT[:, s, :], tpy[s][:, :], ACT.Copy).then_inc(s_yT, 1)

                def sigmoid(g):
                    act.wait_ge(s_gl, g + 1)
                    act.activation(sc[:, g * QT:(g + 1) * QT, :],
                                   gl[g % 2][:, 0, :].rearrange("p (a n) -> p a n", n=E),
                                   ACT.Sigmoid).then_inc(s_sig, 1)

                def weights(g):
                    act.wait_ge(s_tpc, g + 1)
                    act.activation(cwT[:, g, :], gl[g % 2][:, 1, :], ACT.Copy).then_inc(s_cwT, 1)
                    act.wait_ge(s_cwT, g + 1)
                    dst = d["cw"][g].rearrange("e (a k) -> (e a) k", k=P)
                    act.dma_start(dst, cwT[:, g, :]).then_inc(s_cwo, 16)

                def high(u):
                    act.wait_ge(s_w[u % WR], 16 * (u // WR + 1))
                    act.activation(whi[:, u, :], wraw[:, u % WR, :], ACT.Copy).then_inc(s_hi, 1)

                def modulated(b):
                    for s in range(NS):
                        act.wait_ge(s_tpx, NS * b + s + 1)
                        act.activation(t["h2"][:, b, s, :], tpx[s][:, :], ACT.Identity,
                                       scale=t["mod"][:, 8 + s:9 + s],
                                       bias=t["mod"][:, 6 + s:7 + s]).then_inc(s_h2, 1)
                    act.wait_ge(s_x1r, 2 * (b + 1))
                    act.dma_start(d["x1"][b], t["x"][:, TPB * b:TPB * b + TPB, :].rearrange(
                        "p a n -> p (a n)")).then_inc(s_x1, 16)

                for k in range(STEPS):
                    if k < NB:
                        turned(k)
                    if 0 < k <= NB:
                        for u in cuts[k - 1]:
                            high(u)
                    if 0 <= k - 3 < NB:
                        modulated(k - 3)
                    if k >= 5 and k % 2:
                        sigmoid((k - 5) // 2)
                    if k >= 6 and k % 2 == 0:
                        weights((k - 6) // 2)
                act.wait_ge(s_x1, 16 * NB)
                act.wait_ge(s_cwo, 64)

            @block.gpsimd
            def _(pool):
                pool.memset(half[:, :], -0.5).then_inc(s_half, 1)
                pool.wait_ge(s_half, 1)
                for b in range(NB):
                    pool.wait_ge(s_ve, b + 1)
                    pool.tensor_tensor(rstd[:, b % 2, :], ve[:, b % 2, :], half[:, :], ALU.pow).then_inc(s_rstd, 1)
                    for u in cuts[b]:
                        pool.wait_ge(s_hi, u + 1)
                        pool.tensor_tensor(wlo[:, u, :], wraw[:, u % WR, :], whi[:, u, :],
                                           ALU.subtract).then_inc(s_cut, 1)

            @block.vector
            def _(dve):
                n = [0]

                def link(ins):
                    n[0] += 1
                    ins.then_inc(s_dve, 1)
                    dve.wait_ge(s_dve, n[0])

                dve.wait_ge(s_wu, 16)
                for s in range(NS):
                    dve.tensor_tensor(wu[:, s, :], wu[:, s, :], t["gab"][:, 0:D], ALU.mult).then_inc(s_wus, 1)

                def residual(b):
                    for i in range(2):
                        dve.wait_ge(s_pj, 2 * b + i + 1)
                        x = t["x"][:, TPB * b + 2 * i:TPB * b + 2 * i + 2, :]
                        dve.tensor_tensor(x, x, pj[i][:, :].rearrange("p (a n) -> p a n", a=2),
                                          ALU.add).then_inc(s_x1r, 1)
                    dve.wait_ge(s_x1r, 2 * b + 2)
                    for i in range(TPB):
                        ins = dve.bn_stats(stats[:, b % 2, i, :], t["x"][:, TPB * b + i, :])
                    link(ins)
                    for i in range(TPB):
                        ins = dve.bn_aggr(mv[:, b % 2, i, :], stats[:, b % 2, i, :])
                    link(ins)
                    dve.tensor_scalar(ve[:, b % 2, :], mv[:, b % 2, :, 1], EPS, None, ALU.add).then_inc(s_ve, 1)

                def normalised(b):
                    dve.wait_ge(s_rstd, b + 1)
                    if b >= 2:
                        dve.wait_ge(s_tpx, NS * (b - 1))
                    for i in range(TPB):
                        dve.tensor_scalar(xn[:, b % 2, i, :], t["x"][:, TPB * b + i, :], mv[:, b % 2, i, 0:1],
                                          rstd[:, b % 2, i:i + 1], ALU.subtract, ALU.mult).then_inc(s_xn, 1)

                def router(g):
                    score = sc[:, g * QT:(g + 1) * QT, :]
                    for i in range(NG):
                        ins = dve.memset(grank[:, :, i:i + 1], float(NG - 1 - i))
                    link(ins)
                    dve.wait_ge(s_sig, g + 1)
                    dve.wait_ge(s_bias, 16)
                    link(dve.tensor_tensor(sfc[:, :, :], score, bias[:, :].unsqueeze(1).broadcast_to([P, QT, E]),
                                           ALU.add))
                    g4 = sfc[:, :, :].rearrange("p t (g k) -> p t g k", k=E // NG)
                    twos = sfc[:, :, :].rearrange("p t (m k) -> p t m k", k=2)
                    big, small = left[:, :, 0:2 * NG], left[:, :, 2 * NG:4 * NG]
                    dve.tensor_tensor(big, twos[:, :, :, 0], twos[:, :, :, 1], ALU.max)
                    link(dve.tensor_tensor(small, twos[:, :, :, 0], twos[:, :, :, 1], ALU.min))
                    big, small = (v.rearrange("p t (g k) -> p t g k", k=2) for v in (big, small))
                    dve.tensor_tensor(gs[:, :, :], big[:, :, :, 0], big[:, :, :, 1], ALU.max)
                    dve.tensor_tensor(gtmp[:, :, :], big[:, :, :, 0], big[:, :, :, 1], ALU.min)
                    link(dve.tensor_tensor(top[:, :, 0:NG], small[:, :, :, 0], small[:, :, :, 1], ALU.max))
                    link(dve.tensor_tensor(gtmp[:, :, :], gtmp[:, :, :], top[:, :, 0:NG], ALU.max))
                    link(dve.tensor_tensor(gs[:, :, :], gs[:, :, :], gtmp[:, :, :], ALU.add))
                    for k in range(1, NG):
                        n = NG - k
                        link(dve.tensor_tensor(gtmp[:, :, 0:n], gs[:, :, 0:n], gs[:, :, k:NG], ALU.is_ge))
                        link(dve.tensor_tensor(grank[:, :, k:NG], grank[:, :, k:NG], gtmp[:, :, 0:n], ALU.add))
                        link(dve.tensor_tensor(grank[:, :, 0:n], grank[:, :, 0:n], gtmp[:, :, 0:n], ALU.subtract))
                    link(dve.tensor_scalar(gtmp[:, :, :], grank[:, :, :], float(TG) - 0.5, None, ALU.is_lt))
                    keep = gtmp[:, :, :].unsqueeze(3).broadcast_to([P, QT, NG, E // NG])
                    link(dve.tensor_tensor(g4, g4, keep, ALU.mult))
                    link(dve.tensor_scalar(gtmp[:, :, :], gtmp[:, :, :], -1.0, -MASKED, ALU.add, ALU.mult))
                    link(dve.tensor_tensor(g4, g4, keep, ALU.add))
                    for i in range(QT):
                        ins = dve.max(top[:, i, :], sfc[:, i, :])
                    link(ins)
                    link(dve.memset(top[:, :, TOPK:8], MASKED))
                    for i in range(QT):
                        ins = dve.match_replace(left[:, i, :], top[:, i, :], sfc[:, i, :], MASKED)
                    link(ins)
                    link(dve.tensor_tensor(left[:, :, :], sfc[:, :, :], left[:, :, :], ALU.is_gt))
                    link(dve.tensor_tensor(score, score, left[:, :, :], ALU.mult))
                    link(dve.tensor_reduce(wsum[:, :], score, AX_X, ALU.add))
                    link(dve.tensor_scalar(wsum[:, :], wsum[:, :], 1e-20, None, ALU.add))
                    link(dve.reciprocal(wsum[:, :], wsum[:, :]))
                    link(dve.tensor_scalar(wsum[:, :], wsum[:, :], RSCALE, None, ALU.mult))
                    dve.tensor_tensor(cwe[:, g, :].rearrange("p (e a) -> p a e", e=E), score,
                                      wsum[:, :].unsqueeze(2).broadcast_to([P, QT, E]), ALU.mult).then_inc(s_cw, 1)

                for k in range(STEPS):
                    if 0 <= k - 1 < NB:
                        residual(k - 1)
                    if 0 <= k - 2 < NB:
                        normalised(k - 2)
                    if k >= 5 and k % 2:
                        router((k - 5) // 2)

            @block.tensor
            def _(pe):
                def turn(b):
                    for s in range(NS):
                        if b >= 1:
                            pe.wait_ge(s_yT, NS * (b - 1) + s + 1)
                        for i in range(TPB):
                            ins = pe.transpose(tpy[s][:, i * P:(i + 1) * P],
                                               t["y"][:, TPB * b + i, s * P:(s + 1) * P], t["identf"][:, :])
                        ins.then_inc(s_tpy, 1)

                def proj(b):
                    pe.wait_ge(s_yT, NS * (b + 1))
                    for i in range(TPB):
                        if b >= 1 and i % 2 == 0:
                            pe.wait_ge(s_x1r, 2 * (b - 1) + i // 2 + 1)
                        for s in range(NS):
                            ins = pe.matmul(pj[i // 2][:, (i % 2) * D:(i % 2 + 1) * D],
                                            yT[:, s, i * P:(i + 1) * P], wu[:, s, :],
                                            start=(s == 0), stop=(s == NS - 1))
                        if i % 2:
                            ins.then_inc(s_pj, 1)

                def normed(b):
                    pe.wait_ge(s_xn, TPB * (b + 1))
                    for s in range(NS):
                        if b >= 1:
                            pe.wait_ge(s_h2, NS * (b - 1) + s + 1)
                        for i in range(TPB):
                            ins = pe.transpose(tpx[s][:, i * P:(i + 1) * P], xn[:, b % 2, i, s * P:(s + 1) * P],
                                               t["identf"][:, :])
                        ins.then_inc(s_tpx, 1)

                def logits(b):
                    pe.wait_ge(s_h2, NS * (b + 1))
                    if b >= 4:
                        pe.wait_ge(s_cwT, b // 2 - 1)
                    for i in range(TPB):
                        n = b % 2 * TPB + i
                        for s in range(NS):
                            ins = pe.matmul(gl[b // 2 % 2][:, 0, n * E:(n + 1) * E],
                                            t["h2"][:, b, s, i * P:(i + 1) * P], gwT[:, s, :],
                                            start=(s == 0), stop=(s == NS - 1))
                    if b % 2:
                        ins.then_inc(s_gl, 1)

                def weights(g):
                    pe.wait_ge(s_cw, g + 1)
                    pe.transpose(gl[g % 2][:, 1, :], cwe[:, g, :], t["identf"][:, :]).then_inc(s_tpc, 1)

                for k in range(STEPS):
                    if k < NB:
                        turn(k)
                    if k == 1:
                        pe.wait_ge(s_wus, NS)
                        pe.wait_ge(s_gw, 16)
                    if 0 <= k - 1 < NB:
                        proj(k - 1)
                    if 0 <= k - 3 < NB:
                        normed(k - 3)
                    if 0 <= k - 4 < NB:
                        logits(k - 4)
                    if k >= 6 and k % 2 == 0:
                        weights((k - 6) // 2)


HC = E // 4
NQ = 2 * U
EWRAP = 6


def unit_schedule():
    events = []
    for p in range(2):
        s = p * U
        for u in range(U):
            events += [(s + u, "UP", p, u), (s + u + 1, "DOWN", p, u), (s + u, "UNIT", p, u)]
        events += [(s + U, "SUM", p, 0), (s + U + 1, "SCALE", p, 0), (s + U + 2, "BACK", p, 0),
                   (s + U + 4, "RES", p, 0), (s + U + 5, "OUT", p, 0)]
        events += [(s - U + 4, "H", p, 0), (s + 8, "X1", p, 0)]
        events += [(s + at, "CW", p, k) for k, at in enumerate((-6, -2, 4, 8))]
    kinds = ("UP", "DOWN", "UNIT", "SUM", "SCALE", "BACK", "RES", "OUT", "H", "CW", "X1")
    return sorted(events, key=lambda e: (e[0], kinds.index(e[1])))


def experts(nc, t, d):
    pair_events = unit_schedule()
    prologue = [(0, e) for e in pair_events if e[0] < EWRAP]
    epilogue = [(0, e) for e in pair_events if e[0] >= EWRAP]
    turn = sorted(epilogue + [(1, (e[0] + NQ,) + e[1:]) for _, e in prologue], key=lambda x: x[1][0])
    with ExitStack() as ctx:
        def sb(name, shape, dt):
            return ctx.enter_context(nc.sbuf_tensor(name, shape, dt))

        whi, wlo, h2 = t["whi"], t["wlo"], t["h2"]
        hhi = sb("hhi", [P, 2, NS, BW], F32R)
        hlo = sb("hlo", [P, 2, NS, BW], F32R)
        cwb = sb("cwb", [P, 2 * HC, BW], F32)
        sg = sb("sg", [P, 2, BW], F32)
        pr = sb("pr", [P, 2, BW], F32)
        ahi = sb("ahi", [P, 2, BW], F32R)
        alo = sb("alo", [P, 2, BW], F32R)
        x1 = sb("x1b", [P, 2, TPB * D], F32)
        z = sb("z", [P, NS, BW], F32)
        tok = sb("tok4", [1, 2 * U], F32)
        hg = [ctx.enter_context(nc.psum_tensor(f"hg{i}", [P, BW], F32)) for i in range(2)]
        hu = [ctx.enter_context(nc.psum_tensor(f"hu{i}", [P, BW], F32)) for i in range(2)]
        ya = [ctx.enter_context(nc.psum_tensor(f"ya{i}", [P, NS, BW], F32)) for i in range(2)]
        names = ("h_full", "h_high", "gu_full", "silu", "dve_chain", "pr_full", "ahi_done", "act_full", "y_full",
                 "z_add", "z_full", "zt_full", "out_full", "cw_free", "x1_in0", "x1_in1", "cw_in0", "cw_in1",
                 "out_done0", "out_done1")
        q = {n: ctx.enter_context(nc.semaphore("ex_" + n)) for n in names}

        def run(eng, section, free=()):
            led = Ledger(eng, q)
            for name, by in free:
                eng.sem_inc(q[name], by)
                led.raised(name, by)
            led.run(lambda events, pair: section(events, led, pair), prologue, turn, NB // 2 - 1, epilogue)
            return led

        def last_of_load(u):
            return u < E and u % HC == HC - 1

        with nc.Block() as block:
            @block.sync
            def _(sp):
                loads = [0]

                def section(events, led, pair):
                    for ahead, (s, kind, p, k) in events:
                        at = pair + ahead
                        if kind == "UNIT" and last_of_load(k):
                            led.raised("cw_free")
                        elif kind == "CW":
                            loads[0] += 1
                            led.wait("cw_free", loads[0])
                            src = d["cw"][bass.ds(at, 1), k * HC:(k + 1) * HC, p * BW:(p + 1) * BW]
                            sp.dma_start(cwb[:, k % 2 * HC:(k % 2 + 1) * HC, :], src.broadcast_to([P, HC, BW])
                                         ).then_inc(q[f"cw_in{k % 2}"], 16)
                        elif kind == "X1":
                            led.wait(f"out_done{p}")
                            src = d["x1"][bass.ds(at * 2 + p, 1), :, :].rearrange("a p n -> (a p) n")
                            sp.dma_start(x1[:, p, :], src).then_inc(q[f"x1_in{p}"], 16)
                        elif kind == "OUT":
                            led.raised("out_full")
                            led.wait("out_full")
                            dst = d["out"][bass.ds((at * 2 + p) * TPB, TPB), :, :].rearrange("a p n -> p a n")
                            sp.dma_start(dst, x1[:, p, :].rearrange("p (a n) -> p a n", a=TPB)
                                         ).then_inc(q[f"out_done{p}"], 16)
                            led.raised(f"out_done{p}", 16)

                led = run(sp, section, free=(("cw_free", 2), ("out_done0", 16), ("out_done1", 16)))
                led.wait("out_done0")
                led.wait("out_done1")

            @block.tensor
            def _(pe):
                def section(events, led, _):
                    for ahead, (s, kind, p, u) in events:
                        i = u % 2
                        if kind == "H":
                            led.raised("h_full", NS)
                        elif kind == "UP":
                            if u == 0:
                                led.wait("h_full")
                            for k, bank in ((0, hg[i]), (1, hu[i])):
                                m = 0
                                for half in range(NS):
                                    c0 = (k * NS + half) * I
                                    for w, h in ((whi, hhi), (whi, hlo), (wlo, hhi)):
                                        ins = pe.matmul(bank[:, :], w[:, u, c0:c0 + I], h[:, p, half, :],
                                                        start=(m == 0), stop=(m == 5))
                                        m += 1
                            ins.then_inc(q["gu_full"], 1)
                        elif kind == "UNIT":
                            led.raised("act_full")
                        elif kind == "DOWN":
                            led.wait("act_full")
                            for half in range(NS):
                                c0 = 2 * NS * I + half * P
                                for m, (w, a) in enumerate(((whi, ahi), (whi, alo), (wlo, ahi))):
                                    ins = pe.matmul(ya[p][:, half, :], w[:, u, c0:c0 + P], a[:, i, :],
                                                    start=(u == 0 and m == 0), stop=(u == U - 1 and m == 2))
                            if u == U - 1:
                                ins.then_inc(q["y_full"], 1)
                        elif kind == "SCALE":
                            led.raised("z_full", NS)
                        elif kind == "BACK":
                            led.wait("z_full")
                            out = ya[p][:, :, :].rearrange("p s (i n) -> p (s i) n", n=D)
                            for i in range(TPB):
                                for half in range(NS):
                                    ins = pe.transpose(out[:, i, half * P:(half + 1) * P],
                                                       z[:, half, i * P:(i + 1) * P], t["identf"][:, :])
                            ins.then_inc(q["zt_full"], 1)

                run(pe, section)

            @block.scalar
            def _(act):
                def section(events, led, pair):
                    for ahead, (s, kind, p, u) in events:
                        i = u % 2
                        if kind == "UNIT":
                            led.raised("gu_full")
                            led.wait("gu_full")
                            act.activation(sg[:, i, :], hg[i][:, :], ACT.Silu).then_inc(q["silu"], 1)
                            led.raised("pr_full")
                            led.wait("pr_full")
                            act.activation(ahi[:, i, :], pr[:, i, :], ACT.Copy).then_inc(q["ahi_done"], 1)
                            if last_of_load(u):
                                k = p * U + u
                                act.activation(tok[:, k:k + 1], t["mod"][0:1, 0:1],
                                               ACT.Copy).then_inc(q["cw_free"], 1)
                        elif kind == "H":
                            b = (pair + ahead) * 2 + p
                            for half in range(NS):
                                h = h2[:, bass.ds(b, 1), half, :].rearrange("p a n -> p (a n)")
                                act.activation(hhi[:, p, half, :], h, ACT.Copy).then_inc(q["h_high"], 1)
                        elif kind == "SUM":
                            led.raised("z_add", NS)
                        elif kind == "SCALE":
                            led.wait("z_add")
                            for half in range(NS):
                                act.activation(z[:, half, :], z[:, half, :], ACT.Copy, scale=t["gb"][:, half:half + 1]
                                               ).then_inc(q["z_full"], 1)

                run(act, section)

            @block.vector
            def _(dve):
                def section(events, led, pair):
                    for ahead, (s, kind, p, u) in events:
                        i = u % 2
                        if kind == "CW":
                            led.raised(f"cw_in{u % 2}", 16)
                        elif kind == "X1":
                            led.raised(f"x1_in{p}", 16)
                        elif kind == "DOWN" and u == U - 1:
                            led.raised("y_full")
                        elif kind == "BACK":
                            led.raised("zt_full")
                        elif kind == "UNIT":
                            led.raised("silu")
                            led.wait("silu")
                            if u < E:
                                dve.tensor_tensor(sg[:, i, :], sg[:, i, :], hu[i][:, :],
                                                  ALU.mult).then_inc(q["dve_chain"], 1)
                                if u % HC == 0:
                                    led.wait(f"cw_in{u // HC % 2}")
                                led.raised("dve_chain")
                                led.wait("dve_chain")
                                dve.tensor_tensor(pr[:, i, :], sg[:, i, :], cwb[:, u % (2 * HC), :],
                                                  ALU.mult).then_inc(q["pr_full"], 1)
                            else:
                                dve.tensor_tensor(pr[:, i, :], sg[:, i, :], hu[i][:, :],
                                                  ALU.mult).then_inc(q["pr_full"], 1)
                            led.raised("ahi_done")
                            led.wait("ahi_done")
                            dve.tensor_tensor(alo[:, i, :], pr[:, i, :], ahi[:, i, :],
                                              ALU.subtract).then_inc(q["act_full"], 1)
                        elif kind == "H":
                            for half in range(NS):
                                led.raised("h_high")
                                led.wait("h_high")
                                h = h2[:, bass.ds((pair + ahead) * 2 + p, 1), half, :].rearrange("p a n -> p (a n)")
                                dve.tensor_tensor(hlo[:, p, half, :], h, hhi[:, p, half, :],
                                                  ALU.subtract).then_inc(q["h_full"], 1)
                        elif kind == "SUM":
                            led.wait("y_full")
                            for half in range(NS):
                                h = h2[:, bass.ds((pair + ahead) * 2 + p, 1), half, :].rearrange("p a n -> p (a n)")
                                dve.tensor_tensor(z[:, half, :], ya[p][:, half, :], h,
                                                  ALU.add).then_inc(q["z_add"], 1)
                        elif kind == "RES":
                            led.wait("zt_full")
                            led.wait(f"x1_in{p}")
                            dve.tensor_tensor(x1[:, p, :], x1[:, p, :], ya[p][:, :, :].rearrange("p s n -> p (s n)"),
                                              ALU.add).then_inc(q["out_full"], 1)

                run(dve, section)


def build(nc, d):
    with ExitStack() as ctx:
        def sb(c, name, shape, dt):
            return c.enter_context(nc.sbuf_tensor(name, shape, dt))

        t = {}
        t["identf"] = sb(ctx, "identf", [P, P], F32)
        t["mod"] = sb(ctx, "mod", [P, 12], F32)
        t["gb"] = sb(ctx, "gb", [P, NS], F32)
        t["h2"] = sb(ctx, "h2", [P, NB, NS, BW], F32)
        t["y"] = t["h2"][:, :, :, :].rearrange("p b s n -> p (b s n)").rearrange("p (i n) -> p i n", n=D)
        with ExitStack() as mid:
            t["gab"] = sb(mid, "gab", [P, 2 * D], F32)
            t["x"] = sb(mid, "xres", [P, NT, D], F32)
            with ExitStack() as early:
                t["identb"] = sb(early, "identb", [P, P], BF16)
                t["maskq"] = sb(early, "maskq", [P, P], BF16)
                t["maskk"] = sb(early, "maskk", [P, P], BF16)
                t["wbd"] = sb(early, "wbd", [P, 3, P], F32)
                t["v"] = sb(early, "v", [P, NT, HPAD * C], F32)
                t["vpad"] = [sb(early, f"vpad{i}", [P, NT, 32], F32) for i in range(2)]
                t["qst"] = [sb(early, f"qst{i}", [P, T], BF16) for i in range(2)]
                t["kst"] = [sb(early, f"kst{i}", [P, T], BF16) for i in range(2)]
                prepare(nc, t, d)
                attend(nc, t, d)
            for name in ("whi", "wlo"):
                t[name] = ctx.enter_context(nc.sbuf_tensor(name, [P, U, WU], F32R, side="right"))
            project(nc, t, d)
        experts(nc, t, d)


_OUT = ((1, T, D), "float32")


def kernel(**inputs):
    import numpy as _np
    import concourse.bacc as _bacc
    from concourse.bass_utils import run_bass_kernel_spmd as _run

    a = {k: _np.asarray(v) for k, v in inputs.items()}

    def units(w, s):
        both = _np.concatenate([w, s.reshape(2, I, D)], axis=0)
        return both.transpose(0, 2, 1).reshape(U, NS, P, I).transpose(0, 2, 1, 3).reshape(U, P, NS * I)

    down = _np.concatenate([a["L0_ffn_Wd"].transpose(0, 2, 1), a["L0_ffn_Ws_d"].T.reshape(2, I, D)], axis=0)
    arrays = {
        "x": a["L0_attn_x"], "c": a["L0_c"], "wmod": a["L0_wmod"], "bu": a["L0_attn_bu"],
        "wrep": _np.tile(_np.stack([a[f"L0_attn_W{w}"].T for w in "qkv"], axis=1), (P // C, 1, 1)),
        "WuT": a["L0_attn_Wu"].T, "gwT": a["L0_ffn_gate_w"].T, "gbias": a["L0_ffn_gate_bias"],
        "wcat": _np.concatenate([units(a["L0_ffn_Wg"], a["L0_ffn_Ws_g"]),
                                 units(a["L0_ffn_Wu"], a["L0_ffn_Ws_u"]), down], axis=2),
    }
    arrays = {f"in_{k}": _np.ascontiguousarray(v) for k, v in arrays.items()}
    nc = _bacc.Bacc("TRN2", target_bir_lowering=False, num_devices=1)
    d = {k[3:]: nc.dram_tensor(k, v.shape, mybir.dt.from_np(v.dtype), kind="ExternalInput").ap()
         for k, v in arrays.items()}
    for name in ("qs", "ks"):
        d[name] = nc.dram_tensor(name, [3, HPAD * C, T], BF16).ap()
    d["x1"] = nc.dram_tensor("x1", [NB, P, TPB * D], F32).ap()
    d["cw"] = nc.dram_tensor("cw", [NB // 2, E, 2 * BW], F32).ap()
    out = nc.dram_tensor("out_0", _OUT[0], mybir.dt.from_np(_np.dtype(_OUT[1])), kind="ExternalOutput").ap()
    d["out"] = out.rearrange("a (n p) c -> (a n) p c", p=P)
    build(nc, d)
    r = _run(nc, [arrays], core_ids=[0])
    return r.results[0]["out_0"]
```
